# Optimizing a Trainium2 kernel written in Bass

```python
import numpy as np
import jax
import jax.numpy as jnp

def _softmax(x, axis=-1):
    return jax.nn.softmax(x, axis=axis)

def _gelu(x):
    return jax.nn.gelu(x, approximate=True)

def _silu(x):
    return jax.nn.silu(x)

def _sigmoid(x):
    return jax.nn.sigmoid(x)

def _layernorm(x, axis=-1, eps=1e-05):
    m = jnp.mean(x, axis=axis, keepdims=True)
    v = jnp.var(x, axis=axis, keepdims=True)
    return (x - m) / jnp.sqrt(v + eps)

def _scatter_add(tgt, idx, src, axis=0):
    return tgt.at[idx].add(src)

def _segment_sum(src, seg, n):
    return jax.ops.segment_sum(src, seg, n)
kernel_name = 'mk_adj_preln_d2_adj_r2_ccf642'

def setup_inputs(seed: int=0):
    np.random.seed(seed)
    _w = jnp.asarray

    def _rec_inputs():
        import jax
        import jax.numpy as jnp
        _gk = jax.random.key(seed)
        x = -0.0002928 + 1 * jax.random.normal(jax.random.fold_in(_gk, 1), (32, 256, 256), jnp.float32)
        _a = jax.random.bernoulli(jax.random.fold_in(_gk, 2), 0.0078125, (256, 256))
        _a = jnp.logical_or(_a, jnp.swapaxes(_a, -1, -2))
        _a = jnp.logical_or(_a, jnp.eye(256, dtype=bool))
        adj = _a.astype(jnp.int32)
        return (x, adj)
    x, adj = _rec_inputs()

    def _L0_gnn_setup():
        import jax, jax.numpy as jnp
        import numpy as np
        D_MODEL = 256
        NUM_HEADS = 8
        D_HEAD = D_MODEL // NUM_HEADS
        B, N = (4, 1024)
        key = jax.random.key(seed)
        ks = jax.random.split(key, 10)
        s = 1.0 / np.sqrt(D_MODEL)
        inp = {'h': jax.random.normal(ks[0], (B, N, D_MODEL), dtype=jnp.float32), 'adj': jax.random.randint(ks[1], (N, N), 0, 2, dtype=jnp.int32), 'Wq': jax.random.uniform(ks[2], (D_MODEL, D_MODEL), jnp.float32, -s, s), 'bq': jax.random.uniform(ks[3], (D_MODEL,), jnp.float32, -s, s), 'Wk': jax.random.uniform(ks[4], (D_MODEL, D_MODEL), jnp.float32, -s, s), 'bk': jax.random.uniform(ks[5], (D_MODEL,), jnp.float32, -s, s), 'Wv': jax.random.uniform(ks[6], (D_MODEL, D_MODEL), jnp.float32, -s, s), 'bv': jax.random.uniform(ks[7], (D_MODEL,), jnp.float32, -s, s), 'Wo': jax.random.uniform(ks[8], (D_MODEL, D_MODEL), jnp.float32, -s, s), 'bo': jax.random.uniform(ks[9], (D_MODEL,), jnp.float32, -s, s)}
        return inp
    _L0_gnn_all = _L0_gnn_setup()
    _L0_gnn_in = {k: v for k, v in _L0_gnn_all.items() if k in ('Wq', 'bq', 'Wk', 'bk', 'Wv', 'bv', 'Wo', 'bo')}
    del _L0_gnn_all

    def _L1_gnn_setup():
        import jax, jax.numpy as jnp
        import numpy as np
        B, K, DIN, DOUT = (32, 64, 256, 256)
        key = jax.random.key(seed)
        k1, k2, k3, k4 = jax.random.split(key, 4)
        x = jax.random.normal(k1, (B, K, DIN), dtype=jnp.float32)
        adj = jax.random.randint(k2, (K, K), 0, 2, dtype=jnp.int32)
        W = jax.random.normal(k3, (DOUT, 2 * DIN), dtype=jnp.float32) * 0.02
        b = jax.random.normal(k4, (DOUT,), dtype=jnp.float32) * 0.02
        return {'x': x, 'adj': adj, 'W': W, 'b': b}
    _L1_gnn_all = _L1_gnn_setup()
    _L1_gnn_in = {k: v for k, v in _L1_gnn_all.items() if k in ('W', 'b')}
    del _L1_gnn_all
    return {'x': x, 'adj': adj, 'L0_gnn_Wq': _L0_gnn_in['Wq'], 'L0_gnn_bq': _L0_gnn_in['bq'], 'L0_gnn_Wk': _L0_gnn_in['Wk'], 'L0_gnn_bk': _L0_gnn_in['bk'], 'L0_gnn_Wv': _L0_gnn_in['Wv'], 'L0_gnn_bv': _L0_gnn_in['bv'], 'L0_gnn_Wo': _L0_gnn_in['Wo'], 'L0_gnn_bo': _L0_gnn_in['bo'], 'L1_gnn_W': _L1_gnn_in['W'], 'L1_gnn_b': _L1_gnn_in['b']}

def reference(x, adj, L0_gnn_Wq, L0_gnn_bq, L0_gnn_Wk, L0_gnn_bk, L0_gnn_Wv, L0_gnn_bv, L0_gnn_Wo, L0_gnn_bo, L1_gnn_W, L1_gnn_b):
    import jax
    import jax.numpy as jnp

    def _L0_gnn_ref(h, adj, Wq, bq, Wk, bk, Wv, bv, Wo, bo):
        import jax, jax.numpy as jnp
        import numpy as np
        D_MODEL = 256
        NUM_HEADS = 8
        D_HEAD = D_MODEL // NUM_HEADS
        B, N = (4, 1024)
        b, n, _ = h.shape

        def split_heads(x):
            return x.reshape(b, n, NUM_HEADS, D_HEAD).transpose(0, 2, 1, 3)
        q = split_heads(h @ Wq.T + bq)
        k = split_heads(h @ Wk.T + bk)
        v = split_heads(h @ Wv.T + bv)
        scale = 1.0 / np.sqrt(D_HEAD)
        scores = jnp.einsum('bhqd,bhkd->bhqk', q, k) * scale
        mask = (adj == 0)[None, None, :, :]
        scores = jnp.where(mask, -jnp.inf, scores)
        attn = jax.nn.softmax(scores, axis=-1)
        out = jnp.einsum('bhqk,bhkd->bhqd', attn, v)
        out = out.transpose(0, 2, 1, 3).reshape(b, n, D_MODEL)
        return out @ Wo.T + bo

    def _L1_gnn_ref(x, adj, W, b):
        import jax, jax.numpy as jnp
        import numpy as np
        B, K, DIN, DOUT = (32, 64, 256, 256)
        Din = x.shape[-1]
        Wi, Wj = (W[:, :Din], W[:, Din:])
        mi = jnp.einsum('bkd,od->bko', x, Wi)
        mj = jnp.einsum('bkd,od->bko', x, Wj)
        a = adj.astype(x.dtype)
        deg = a.sum(axis=1)
        out = deg[None, :, None] * (mi + b) + jnp.einsum('ij,bjo->bio', a, mj)
        return out
    h = jnp.maximum(_layernorm(x, axis=-1), 0.0)
    x = x + _L0_gnn_ref(h, adj, L0_gnn_Wq, L0_gnn_bq, L0_gnn_Wk, L0_gnn_bk, L0_gnn_Wv, L0_gnn_bv, L0_gnn_Wo, L0_gnn_bo)
    h = jnp.maximum(_layernorm(x, axis=-1), 0.0)
    x = x + _L1_gnn_ref(h, adj, L1_gnn_W, L1_gnn_b)
    return x

_drawn_inputs = setup_inputs


def setup_inputs(seed=0):
    import zlib

    import numpy as np

    out = dict(_drawn_inputs(seed))
    spreads = {}
    factors = {'L0_gnn_Wq': 6.068,
     'L0_gnn_bq': 8.0,
     'L0_gnn_Wk': 5.908,
     'L0_gnn_bk': 8.0,
     'L0_gnn_bv': 2.725}
    for name, (base, spread) in spreads.items():
        noise = np.random.default_rng([zlib.crc32(name.encode()), seed]).standard_normal(out[name].shape)
        drawn = base * np.exp(spread * noise) if base else spread * noise
        out[name] = jnp.asarray(drawn.astype(out[name].dtype))
    for name, factor in factors.items():
        out[name] = (out[name] * factor).astype(out[name].dtype)
    return out
```

```python
from contextlib import ExitStack

import concourse.bass as bass
from concourse import mybir

F32 = mybir.dt.float32
F32R = mybir.dt.float32r
I32 = mybir.dt.int32
ALU = mybir.AluOpType
ACT = mybir.ActivationFunctionType
AX_X = mybir.AxisListType.X

P = 128
LN_EPS = 1e-5
MASKED = 1e30
N_DMA = 16


def graph_layers(nc, x, WqT, WkT, WvT, WoT, WiT, WjT, bq, bk, bv, bo, b1, adj, adjT, ident, out):
    B, N, D = x.shape
    TT = N // P
    FC = D // P
    HD = 32
    H = D // HD
    HC = P // HD
    SCALE = float(HD) ** -0.5
    assert TT == 2 and FC == 2 and N == 256 and D == 256

    x_t = x.rearrange("b (t p) f -> b p t f", p=P)
    out_t = out.rearrange("b (t p) f -> b p t f", p=P)

    with ExitStack() as ctx:
        def sb(name, shape, dt=F32):
            return ctx.enter_context(nc.sbuf_tensor(name, shape, dt))

        def ps(name, shape):
            return ctx.enter_context(nc.psum_tensor(name, shape, F32))

        def sem(name):
            return ctx.enter_context(nc.semaphore(name))

        wq, wk, wv, wo, wi, wj = (sb(n, [P, FC, D]) for n in ("wq", "wk", "wv", "wo", "wi", "wj"))
        wq_raw = sb("wq_raw", [P, FC, D])
        bq_raw = sb("bq_raw", [P, FC])
        bq_s = sb("bq_s", [P, FC])
        bk_s = sb("bk_s", [P, FC])
        bv_s = sb("bv_s", [P, FC])
        bv_rep = sb("bv_rep", [P, FC, P])
        bo_rows = sb("bo_rows", [P, D])
        b1_rows = sb("b1_rows", [P, D])
        adj_i = sb("adj_i", [P, TT, N], I32)
        adjT_i = sb("adjT_i", [P, TT, N], I32)
        adj_f = sb("adj_f", [P, TT, N])
        adjT_f = sb("adjT_f", [P, TT, N])
        mask = sb("mask", [P, TT, N])
        deg = sb("deg", [P, TT])
        out_bias = sb("out_bias", [P, TT, D])
        deg_bias = sb("deg_bias", [P, TT, D])
        idn = sb("idn", [P, P])
        minus_half = sb("minus_half", [P, TT])

        X = [sb(f"X_{i}", [P, TT, D]) for i in range(2)]
        XB = [sb(f"XB_{i}", [P, TT, D]) for i in range(2)]
        bn1 = sb("bn1", [P, TT, 6])
        mv1 = sb("mv1", [P, TT, 2])
        ve1 = sb("ve1", [P, TT])
        rs1 = sb("rs1", [P, TT])
        XN = sb("XN", [P, TT, D])
        HT = sb("HT", [P, FC, N])
        Qhi = sb("Qhi", [P, FC, N], F32R)
        Qlo = sb("Qlo", [P, FC, N], F32R)
        Khi = sb("Khi", [P, FC, N], F32R)
        Klo = sb("Klo", [P, FC, N], F32R)
        QS = [sb(f"QS_{i}", [P, HC, FC, N], F32R) for i in range(2)]
        KS = [sb(f"KS_{i}", [P, HC, FC, N], F32R) for i in range(2)]
        V = [sb(f"V_{i}", [P, TT, D]) for i in range(2)]
        NSM = 4
        SM = sb("SM", [P, NSM, TT, N])
        PR = sb("PR", [P, NSM, TT, N])
        MN = [sb(f"MN_{i}", [P, H, TT]) for i in range(2)]
        DEN = [sb(f"DEN_{i}", [P, H, TT]) for i in range(2)]
        RD = sb("RD", [P, H, TT])
        RDX = sb("RDX", [P, TT, H, HD])
        PT = sb("PT", [P, H, TT, N])
        RS = sb("RS", [P, FC, N])
        OT = sb("OT", [P, FC, N])
        X1 = sb("X1", [P, TT, D])
        X1B = sb("X1B", [P, TT, D])
        bn2 = sb("bn2", [P, TT, 6])
        mv2 = sb("mv2", [P, TT, 2])
        ve2 = sb("ve2", [P, TT])
        rs2 = sb("rs2", [P, TT])
        XN2 = sb("XN2", [P, TT, D])
        GT = sb("GT", [P, FC, N])
        MJ = sb("MJ", [P, TT, D])
        MIB = sb("MIB", [P, TT, D])
        OUT = [sb(f"OUT_{i}", [P, TT, D]) for i in range(2)]

        S_ps = [ps(f"S_ps_{i}", [P, TT, N]) for i in range(2)]
        PT_ps = [ps(f"PT_ps_{i}", [P, TT, N]) for i in range(2)]
        O_ps = ps("O_ps", [P, FC, N])
        G_ps = [ps(f"G_ps_{i}", [P, 2, N]) for i in range(3)]

        consts_loaded = sem("consts_loaded")
        setup_dve = sem("setup_dve")
        setup_pe = sem("setup_pe")
        setup_pool = sem("setup_pool")
        x_loaded = [sem(f"x_loaded_{i}") for i in range(2)]
        stacked = [sem(f"stacked_{i}") for i in range(2)]
        stored = [sem(f"stored_{i}") for i in range(2)]
        ht_mm, q_mm, k_mm, v_mm, s_mm, t_mm, o_mm, r_mm, y_mm, gt_mm, mi_mm, mj_mm, a_mm = (
            sem(f"{n}_mm") for n in ("ht", "q", "k", "v", "s", "t", "o", "r", "y", "gt", "mi", "mj", "a"))
        qhi_ok, khi_ok, v_ok, exp_ok, pt_ok, r_ok, mj_ok = (
            sem(n) for n in ("qhi_ok", "khi_ok", "v_ok", "exp_ok", "pt_ok", "r_ok", "mj_ok"))
        st1_ok, ht_ok, qlo_ok, klo_ok, min_ok, rd_ok, ot_ok, x1_ok, st2_ok, xn2_ok, gt_ok, mib_ok, out_ok = (
            sem(n) for n in ("st1_ok", "ht_ok", "qlo_ok", "klo_ok", "min_ok", "rd_ok", "ot_ok", "x1_ok",
                             "st2_ok", "xn2_ok", "gt_ok", "mib_ok", "out_ok"))
        dve_bn1, dve_mv1, dve_bn2, dve_mv2, dve_rd = (
            sem(n) for n in ("dve_bn1", "dve_mv1", "dve_bn2", "dve_mv2", "dve_rd"))
        dve_passed, pool_passed = sem("dve_passed"), sem("pool_passed")
        rs1_ok, xn1_ok, xb_ok, rs2_ok, x1b_ok = (
            sem(n) for n in ("rs1_ok", "xn1_ok", "xb_ok", "rs2_ok", "x1b_ok"))

        N_CONST = 14
        SETUP_DVE = 9
        N_STACK = 6 * HC

        def uses(half, p, k):
            return half + (p + k) // 2 + 1

        def wait(eng, s, value):
            if isinstance(value, int) and value <= 0:
                return
            eng.wait_ge(s, value)

        def stand_alone(eng, passed):
            eng.sem_inc(passed, 1)

        def pipeline(eng, step):
            def one(g):
                step(g, g // 2, g % 2, tuple(0 <= g + k < B for k in (2, 1, 0, -1, -2)))
            first, pairs = 3, (B - 5) // 2
            for g in range(-2, first):
                one(g)
            with eng.Fori(0, pairs) as i:
                step(2 * i + first, i + 1, 1, (True,) * 5)
                step(2 * i + first + 1, i + 2, 0, (True,) * 5)
            for g in range(first + 2 * pairs, B + 2):
                one(g)

        block = ctx.enter_context(nc.Block())

        @block.sync
        def _(sp):
            for tile, src in ((wq_raw, WqT), (wk, WkT), (wv, WvT), (wo, WoT), (wi, WiT), (wj, WjT)):
                sp.dma_start(tile[:], src.rearrange("(c p) o -> p c o", p=P)).then_inc(consts_loaded, N_DMA)
            for tile, src in ((bq_raw, bq), (bk_s, bk), (bv_s, bv)):
                sp.dma_start(tile[:], src).then_inc(consts_loaded, N_DMA)
            for tile, src in ((bo_rows, bo), (b1_rows, b1)):
                sp.dma_start(tile[:], src.rearrange("(a f) -> a f", a=1).to_broadcast([P, D])
                             ).then_inc(consts_loaded, N_DMA)
            for tile, src in ((adj_i, adj), (adjT_i, adjT)):
                sp.dma_start(tile[:], src.rearrange("(t p) n -> p t n", p=P)).then_inc(consts_loaded, N_DMA)
            sp.dma_start(idn[:], ident).then_inc(consts_loaded, N_DMA)

            def step(g, half, p, parts):
                norm1, project, attend, finish, emit = parts
                if emit:
                    sp.wait_ge(out_ok, g - 1)
                    sp.dma_start(out_t[g - 2], OUT[p][:]).then_inc(stored[p], N_DMA)
                if norm1:
                    wait(sp, xn1_ok, g + 1)
                    wait(sp, xb_ok, g + 1)
                    sp.dma_start(X[p][:], x_t[g + 2]).then_inc(x_loaded[p], N_DMA)
                if project:
                    wait(sp, s_mm, H * g)
                    sp.wait_ge(qhi_ok, g + 2)
                    sp.wait_ge(qlo_ok, g + 2)
                    dst = QS[1 - p]
                    for row, src in enumerate((Qhi, Qlo, Qhi)):
                        for a in range(HC):
                            sp.dma_start(dst[HD * row:HD * row + HD, a].bitcast(F32), src[HD * a:HD * a + HD].bitcast(F32)
                                         ).then_inc(stacked[1 - p], N_DMA)
                    sp.wait_ge(khi_ok, g + 2)
                    sp.wait_ge(klo_ok, g + 2)
                    dst = KS[1 - p]
                    for row, src in enumerate((Khi, Khi, Klo)):
                        for a in range(HC):
                            sp.dma_start(dst[HD * row:HD * row + HD, a].bitcast(F32), src[HD * a:HD * a + HD].bitcast(F32)
                                         ).then_inc(stacked[1 - p], N_DMA)

            pipeline(sp, step)
            for i in range(2):
                sp.wait_ge(stored[i], N_DMA * (B // 2))

        @block.gpsimd
        def _(pool):
            pool.memset(minus_half[:], -0.5).then_inc(setup_pool, 1)
            pool.wait_ge(setup_pool, 1)
            pool.wait_ge(setup_dve, SETUP_DVE)

            def step(g, half, p, parts):
                norm1, project, attend, finish, emit = parts
                if finish:
                    pool.wait_ge(st2_ok, g)
                    pool.tensor_tensor(rs2[:], ve2[:], minus_half[:], ALU.pow).then_inc(rs2_ok, 1)
                    wait(pool, mib_ok, g - 1)
                    pool.tensor_tensor(X1B[:], X1[:], deg_bias[:], ALU.add).then_inc(x1b_ok, 1)
                if project:
                    wait(pool, x1_ok, g)
                    pool.wait_ge(x_loaded[1 - p], N_DMA * uses(half, p, 1))
                    pool.tensor_tensor(XB[1 - p][:], X[1 - p][:], out_bias[:], ALU.add).then_inc(xb_ok, 1)
                if norm1:
                    pool.wait_ge(st1_ok, g + 3)
                    pool.tensor_tensor(rs1[:], ve1[:], minus_half[:], ALU.pow).then_inc(rs1_ok, 1)
                    pool.wait_ge(rs1_ok, g + 3)
                    wait(pool, ht_mm, g + 2)
                    stand_alone(pool, pool_passed)
                    for t in range(TT):
                        last = pool.tensor_scalar(XN[:, t], X[p][:, t], mv1[:, t, 0:1], rs1[:, t:t + 1],
                                                  ALU.subtract, ALU.mult)
                    last.then_inc(xn1_ok, 1)

            pipeline(pool, step)

        @block.scalar
        def _(act):
            act.wait_ge(consts_loaded, N_DMA * N_CONST)
            act.wait_ge(setup_dve, 2)

            def exps(g, p, h):
                act.wait_ge(min_ok, H * g + h + 1)
                wait(act, t_mm, H * g + h + 1 - NSM)
                if h == 0:
                    wait(act, rd_ok, g - 1)
                for t in range(TT):
                    last = act.activation(PR[:, h % NSM, t], SM[:, h % NSM, t], ACT.Exp, scale=-1.0,
                                          bias=MN[p][:, h, t:t + 1], accum_out=DEN[p][:, h, t:t + 1])
                last.then_inc(exp_ok, 1)

            def pt_copy(g, h):
                if h % HC == 0:
                    wait(act, o_mm, FC * (g - 1) + h // HC + 1)
                act.wait_ge(t_mm, H * g + h + 1)
                act.activation(PT[:, h], PT_ps[h % 2][:], ACT.Copy).then_inc(pt_ok, 1)

            def hi_part(g, half, p, dst, src, bias, mm, ok, first):
                act.wait_ge(mm, g + 2)
                if first:
                    wait(act, stacked[p], N_DMA * N_STACK * uses(half, p, 0))
                for c in range(FC):
                    last = act.activation(dst[:, c], src[:, c], ACT.Identity, bias=bias[:, c:c + 1])
                last.then_inc(ok, 1)

            def step(g, half, p, parts):
                norm1, project, attend, finish, emit = parts
                for h in range(H):
                    if attend:
                        exps(g, p, h)
                    if h < 2 and finish:
                        pt_copy(g - 1, H - 2 + h)
                    if h >= 2 and attend:
                        pt_copy(g, h - 2)
                    if h == 1 and project:
                        hi_part(g, half, p, Qhi, G_ps[1], bq_s, q_mm, qhi_ok, True)
                    if h == 2 and finish:
                        act.wait_ge(r_mm, g)
                        wait(act, ot_ok, g - 1)
                        act.activation(RS[:], G_ps[2][:], ACT.Copy).then_inc(r_ok, 1)
                    if h == 3 and project:
                        hi_part(g, half, p, Khi, G_ps[0], bk_s, k_mm, khi_ok, False)
                    if h == 4 and project:
                        act.wait_ge(v_mm, g + 2)
                        wait(act, o_mm, FC * g)
                        act.activation(V[1 - p][:], G_ps[1][:], ACT.Copy).then_inc(v_ok, 1)
                    if h == 7 and finish:
                        act.wait_ge(mj_mm, g)
                        wait(act, a_mm, g - 1)
                        act.activation(MJ[:], G_ps[2][:], ACT.Copy).then_inc(mj_ok, 1)

            pipeline(act, step)

        @block.vector
        def _(dve):
            dve.wait_ge(consts_loaded, N_DMA * N_CONST)
            dve.tensor_scalar(wq[:], wq_raw[:], -SCALE, None, ALU.mult).then_inc(setup_dve, 1)
            dve.tensor_scalar(bq_s[:], bq_raw[:], -SCALE, None, ALU.mult).then_inc(setup_dve, 1)
            for c in range(FC):
                last = dve.tensor_copy(bv_rep[:, c], bv_s[:, c:c + 1].to_broadcast([P, P]))
            last.then_inc(setup_dve, 1)
            dve.tensor_copy(adj_f[:], adj_i[:]).then_inc(setup_dve, 1)
            dve.tensor_copy(adjT_f[:], adjT_i[:]).then_inc(setup_dve, 1)
            for s in range(2):
                dve.memset(QS[s][3 * HD:].bitcast(F32), 0.0)
                last = dve.memset(KS[s][3 * HD:].bitcast(F32), 0.0)
            last.then_inc(setup_dve, 1)
            dve.wait_ge(setup_dve, 6)
            dve.tensor_scalar(mask[:], adj_f[:], 0.0, MASKED, ALU.is_equal, ALU.mult).then_inc(setup_dve, 1)
            dve.tensor_reduce(deg[:], adj_f[:], AX_X, ALU.add).then_inc(setup_dve, 1)
            dve.wait_ge(setup_dve, 8)
            dve.wait_ge(setup_pe, 1)
            for t in range(TT):
                dve.tensor_tensor(out_bias[:, t], G_ps[0][:, 0], bo_rows[:], ALU.add)
                last = dve.tensor_scalar(deg_bias[:, t], b1_rows[:], deg[:, t:t + 1], None, ALU.mult)
            last.then_inc(setup_dve, 1)
            dve.wait_ge(setup_dve, SETUP_DVE)

            def row_minima(g, p, h):
                dve.wait_ge(s_mm, H * g + h + 1)
                wait(dve, exp_ok, H * g + h + 1 - NSM)
                stand_alone(dve, dve_passed)
                for t in range(TT):
                    last = dve.tensor_tensor_reduce(
                        out=SM[:, h % NSM, t], in0=S_ps[h % 2][:, t], in1=mask[:, t], scale=1.0, scalar=3e38,
                        op0=ALU.add, op1=ALU.min, accum_out=MN[p][:, h, t:t + 1])
                last.then_inc(min_ok, 1)

            def lo_part(g, half, p, dst, hi, src, bias, hi_ok, ok):
                dve.wait_ge(hi_ok, g + 2)
                for c in range(FC):
                    last = dve.scalar_tensor_tensor(out=dst[:, c], in0=src[:, c], scalar=bias[:, c:c + 1],
                                                    in1=hi[:, c].bitcast(F32), op0=ALU.add, op1=ALU.subtract)
                last.then_inc(ok, 1)

            def statistics(n, src, bn, mv, ve, bn_sem, mv_sem, ok):
                for t in range(TT):
                    last = dve.bn_stats(bn[:, t], src[:, t])
                last.then_inc(bn_sem, 1)
                dve.wait_ge(bn_sem, n + 1)
                stand_alone(dve, dve_passed)
                for t in range(TT):
                    last = dve.bn_aggr(mv[:, t], bn[:, t])
                last.then_inc(mv_sem, 1)
                dve.wait_ge(mv_sem, n + 1)
                dve.tensor_scalar(ve[:], mv[:, :, 1], LN_EPS, None, ALU.add).then_inc(ok, 1)

            def step(g, half, p, parts):
                norm1, project, attend, finish, emit = parts
                for h in range(H):
                    if attend:
                        row_minima(g, p, h)
                    if h == 0 and emit:
                        dve.wait_ge(mi_mm, g - 1)
                        dve.wait_ge(x1b_ok, g - 1)
                        for t in range(TT):
                            last = dve.scalar_tensor_tensor(out=MIB[:, t], in0=G_ps[1][:, t],
                                                            scalar=deg[:, t:t + 1], in1=X1B[:, t],
                                                            op0=ALU.mult, op1=ALU.add)
                        last.then_inc(mib_ok, 1)
                    if h == 0 and project:
                        dve.wait_ge(ht_mm, g + 2)
                        wait(dve, v_mm, g + 1)
                        dve.tensor_scalar(HT[:], G_ps[0][:], 0.0, None, ALU.max).then_inc(ht_ok, 1)
                    if h == 1 and emit:
                        dve.wait_ge(mib_ok, g - 1)
                        dve.wait_ge(a_mm, g - 1)
                        wait(dve, stored[p], N_DMA * (uses(half, p, -2) - 1))
                        dve.tensor_tensor(OUT[p][:], G_ps[2][:], MIB[:], ALU.add).then_inc(out_ok, 1)
                    if h == 1 and finish:
                        dve.wait_ge(exp_ok, H * g)
                        dve.reciprocal(RD[:], DEN[1 - p][:]).then_inc(dve_rd, 1)
                        dve.wait_ge(dve_rd, g)
                        wait(dve, r_mm, g - 1)
                        for t in range(TT):
                            last = dve.tensor_copy(
                                RDX[:, t], RD[:, :, t:t + 1].to_broadcast([P, H, HD]))
                        last.then_inc(rd_ok, 1)
                    if h == 2 and project:
                        lo_part(g, half, p, Qlo, Qhi, G_ps[1], bq_s, qhi_ok, qlo_ok)
                    if h == 3 and finish:
                        dve.wait_ge(r_ok, g)
                        dve.wait_ge(o_mm, FC * g)
                        wait(dve, y_mm, g - 1)
                        dve.tensor_tensor(OT[:], O_ps[:], RS[:], ALU.mult).then_inc(ot_ok, 1)
                    if h == 4 and finish:
                        dve.wait_ge(y_mm, g)
                        dve.wait_ge(xb_ok, g)
                        wait(dve, x1b_ok, g - 1)
                        dve.tensor_tensor(X1[:], G_ps[2][:], XB[1 - p][:], ALU.add).then_inc(x1_ok, 1)
                        dve.wait_ge(x1_ok, g)
                        statistics(g - 1, X1, bn2, mv2, ve2, dve_bn2, dve_mv2, st2_ok)
                    if h == 4 and project:
                        lo_part(g, half, p, Klo, Khi, G_ps[0], bk_s, khi_ok, klo_ok)
                    if h == 5 and finish:
                        dve.wait_ge(rs2_ok, g)
                        wait(dve, gt_mm, g - 1)
                        for t in range(TT):
                            last = dve.tensor_scalar(XN2[:, t], X1[:, t], mv2[:, t, 0:1], rs2[:, t:t + 1],
                                                     ALU.subtract, ALU.mult)
                        last.then_inc(xn2_ok, 1)
                    if h == 5 and norm1:
                        dve.wait_ge(x_loaded[p], N_DMA * uses(half, p, 2))
                        wait(dve, xn1_ok, g + 2)
                        statistics(g + 2, X[p], bn1, mv1, ve1, dve_bn1, dve_mv1, st1_ok)
                    if h == 6 and finish:
                        dve.wait_ge(gt_mm, g)
                        wait(dve, mi_mm, g - 1)
                        dve.tensor_scalar(GT[:], G_ps[0][:], 0.0, None, ALU.max).then_inc(gt_ok, 1)

            pipeline(dve, step)

        @block.tensor
        def _(pe):
            pe.wait_ge(consts_loaded, N_DMA * N_CONST)
            pe.wait_ge(setup_dve, 3)
            for c in range(FC):
                last = pe.matmul(G_ps[0][:, 0], bv_rep[:, c], wo[:, c], start=(c == 0), stop=(c == FC - 1))
            last.then_inc(setup_pe, 1)
            pe.wait_ge(setup_dve, SETUP_DVE)

            def by_feature(dst, w, src, mm):
                for c in range(FC):
                    for k in range(FC):
                        last = pe.matmul(dst[:, c], w[:, k, P * c:P * c + P], src[:, k],
                                         start=(k == 0), stop=(k == FC - 1))
                last.then_inc(mm, 1)

            def by_token(dst, src, w, mm):
                for t in range(TT):
                    for k in range(FC):
                        last = pe.matmul(dst[:, t], src[:, k, P * t:P * t + P], w[:, k],
                                         start=(k == 0), stop=(k == FC - 1))
                last.then_inc(mm, 1)

            def turn(dst, src, mm):
                for c in range(FC):
                    for t in range(TT):
                        last = pe.transpose(dst[:, c, P * t:P * t + P], src[:, t, P * c:P * c + P], idn[:])
                last.then_inc(mm, 1)

            def bank_read(g, finish_ok, project_ok):
                wait(pe, finish_ok, g - 1)
                if isinstance(g, int) and g < 2:
                    wait(pe, project_ok, g + 1)

            def scores(g, half, p, h):
                if h == 0:
                    pe.wait_ge(stacked[p], N_DMA * N_STACK * uses(half, p, 0))
                wait(pe, min_ok, H * g + h - 1)
                a, c = h % HC, h // HC
                for t in range(TT):
                    last = pe.matmul(S_ps[h % 2][:, t], QS[p][:, a, c, P * t:P * t + P], KS[p][:, a, c],
                                     start=True, stop=True)
                last.then_inc(s_mm, 1)

            def turn_probs(g, h):
                pe.wait_ge(exp_ok, H * g + h + 1)
                wait(pe, pt_ok, H * g + h - 1)
                for k in range(TT):
                    for t in range(TT):
                        last = pe.transpose(PT_ps[h % 2][:, k, P * t:P * t + P],
                                            PR[:, h % NSM, t, P * k:P * k + P], idn[:])
                last.then_inc(t_mm, 1)

            def weigh(g, p, c):
                pe.wait_ge(pt_ok, H * g + HC * (c + 1))
                if c == 0:
                    pe.wait_ge(v_ok, g + 1)
                    wait(pe, ot_ok, g)
                for k in range(TT):
                    for a in range(HC):
                        h = HC * c + a
                        last = pe.matmul(O_ps[HD * a:HD * a + HD, c], V[p][:, k, HD * h:HD * h + HD], PT[:, h, k],
                                         start=(k == 0), stop=(k == TT - 1))
                last.then_inc(o_mm, 1)

            def step(g, half, p, parts):
                norm1, project, attend, finish, emit = parts
                for h in range(H):
                    if attend:
                        scores(g, half, p, h)
                    if h < 2 and finish:
                        turn_probs(g - 1, H - 2 + h)
                    if h >= 2 and attend:
                        turn_probs(g, h - 2)
                    if h == 0 and emit:
                        pe.wait_ge(mj_ok, g - 1)
                        by_token(G_ps[2], adjT_f, MJ, a_mm)
                    if h == 0 and project:
                        pe.wait_ge(xn1_ok, g + 2)
                        bank_read(g, gt_ok, klo_ok)
                        turn(G_ps[0], XN, ht_mm)
                    if h == 1 and project:
                        pe.wait_ge(ht_ok, g + 2)
                        bank_read(g, mib_ok, v_ok)
                        by_feature(G_ps[1], wq, HT, q_mm)
                    if h == 2 and finish:
                        pe.wait_ge(rd_ok, g)
                        wait(pe, out_ok, g - 1)
                        for c in range(FC):
                            for t in range(TT):
                                last = pe.transpose(G_ps[2][:, c, P * t:P * t + P],
                                                    RDX[:, t, HC * c:HC * c + HC], idn[:])
                        last.then_inc(r_mm, 1)
                        weigh(g - 1, 1 - p, 1)
                    if h == 3 and project:
                        by_feature(G_ps[0], wk, HT, k_mm)
                    if h == 3 and finish:
                        pe.wait_ge(ot_ok, g)
                        by_token(G_ps[2], OT, wo, y_mm)
                    if h == 4 and project:
                        pe.wait_ge(qlo_ok, g + 2)
                        by_token(G_ps[1], HT, wv, v_mm)
                    if h == 5 and finish:
                        pe.wait_ge(xn2_ok, g)
                        if project:
                            pe.wait_ge(klo_ok, g + 2)
                        turn(G_ps[0], XN2, gt_mm)
                    if h == 6 and attend:
                        weigh(g, p, 0)
                    if h == 6 and finish:
                        pe.wait_ge(gt_ok, g)
                        pe.wait_ge(x1_ok, g)
                        by_token(G_ps[2], GT, wj, mj_mm)
                    if h == 7 and finish:
                        if project:
                            pe.wait_ge(v_ok, g + 2)
                        by_token(G_ps[1], GT, wi, mi_mm)

            pipeline(pe, step)


def kernel(x, adj, L0_gnn_Wq, L0_gnn_bq, L0_gnn_Wk, L0_gnn_bk, L0_gnn_Wv, L0_gnn_bv, L0_gnn_Wo, L0_gnn_bo,
           L1_gnn_W, L1_gnn_b):
    import numpy as np
    import concourse.bacc as bacc
    from concourse.bass_utils import run_bass_kernel_spmd

    def laid(a):
        return np.ascontiguousarray(np.asarray(a))

    D = x.shape[2]
    W1 = np.asarray(L1_gnn_W)

    def by_partition(b):
        return laid(np.asarray(b).reshape(D // P, P).T)

    arrays = {
        "x": laid(x),
        "WqT": laid(np.asarray(L0_gnn_Wq).T), "WkT": laid(np.asarray(L0_gnn_Wk).T),
        "WvT": laid(np.asarray(L0_gnn_Wv).T), "WoT": laid(np.asarray(L0_gnn_Wo).T),
        "WiT": laid(W1[:, :D].T), "WjT": laid(W1[:, D:].T),
        "bq": by_partition(L0_gnn_bq), "bk": by_partition(L0_gnn_bk), "bv": by_partition(L0_gnn_bv),
        "bo": laid(L0_gnn_bo), "b1": laid(L1_gnn_b),
        "adj": laid(adj), "adjT": laid(np.asarray(adj).T),
        "ident": np.eye(P, dtype=np.float32),
    }
    nc = bacc.Bacc("TRN2", target_bir_lowering=False, num_devices=1)
    args = [nc.dram_tensor(f"in_{n}", a.shape, mybir.dt.from_np(a.dtype), kind="ExternalInput").ap()
            for n, a in arrays.items()]
    out = nc.dram_tensor("out", x.shape, F32, kind="ExternalOutput").ap()
    graph_layers(nc, *args, out)
    r = run_bass_kernel_spmd(nc, [{f"in_{n}": a for n, a in arrays.items()}], core_ids=[0])
    return r.results[0]["out"]
```

```python
from contextlib import ExitStack

import concourse.bass as bass
from concourse import mybir

F32 = mybir.dt.float32
F32R = mybir.dt.float32r
I32 = mybir.dt.int32
ALU = mybir.AluOpType
ACT = mybir.ActivationFunctionType
AX_X = mybir.AxisListType.X

P = 128
LN_EPS = 1e-5
MASKED = 1e30
N_DMA = 16


def graph_layers(nc, x, WqT, WkT, WvT, WoT, WiT, WjT, bq, bk, bv, bo, b1, adj, adjT, ident, out):
    B, N, D = x.shape
    TT = N // P
    FC = D // P
    HD = 32
    H = D // HD
    HC = P // HD
    SCALE = float(HD) ** -0.5
    assert TT == 2 and FC == 2 and N == 256 and D == 256

    x_t = x.rearrange("b (t p) f -> b p t f", p=P)
    out_t = out.rearrange("b (t p) f -> b p t f", p=P)

    with ExitStack() as ctx:
        def sb(name, shape, dt=F32):
            return ctx.enter_context(nc.sbuf_tensor(name, shape, dt))

        def ps(name, shape):
            return ctx.enter_context(nc.psum_tensor(name, shape, F32))

        def sem(name):
            return ctx.enter_context(nc.semaphore(name))

        w_raw = [sb(f"w_raw_{n}", [P, FC, D]) for n in ("q", "k", "v", "o", "i", "j")]
        weights = [sb(f"w_{n}", [P, 2, FC, D], F32R) for n in ("q", "k", "v", "o", "i", "j")]
        wq, wk, wv, wo, wi, wj = weights
        wq_scaled = sb("wq_scaled", [P, FC, D])
        bq_raw = sb("bq_raw", [P, FC])
        bq_s = sb("bq_s", [P, FC])
        bk_s = sb("bk_s", [P, FC])
        bv_s = sb("bv_s", [P, FC])
        bv_rep = sb("bv_rep", [P, FC, P])
        bo_rows = sb("bo_rows", [P, D])
        b1_rows = sb("b1_rows", [P, D])
        adj_i = sb("adj_i", [P, TT, N], I32)
        adjT_i = sb("adjT_i", [P, TT, N], I32)
        adj_f = sb("adj_f", [P, TT, N])
        adjT_r = sb("adjT_r", [P, TT, N], F32R)
        mask = sb("mask", [P, TT, N])
        deg = sb("deg", [P, TT])
        out_bias = sb("out_bias", [P, TT, D])
        deg_bias = sb("deg_bias", [P, TT, D])
        idn = sb("idn", [P, P])
        minus_half = sb("minus_half", [P, TT])

        def two(name, shape, dt=F32):
            return [sb(f"{name}_{i}", shape, dt) for i in range(2)]

        X = two("X", [P, TT, D])
        bn1, mv1 = two("bn1", [P, TT, 6]), two("mv1", [P, TT, 2])
        ve1, rs1 = two("ve1", [P, TT]), two("rs1", [P, TT])
        XN = two("XN", [P, TT, D])
        HT = two("HT", [P, 2, FC, N], F32R)
        Q = sb("Q", [P, 2, FC, N], F32R)
        K = sb("K", [P, 2, FC, N], F32R)
        QS = two("QS", [P, HC, FC, N], F32R)
        KS = two("KS", [P, HC, FC, N], F32R)
        V = two("V", [P, TT, D])
        NSM = 4
        SM = sb("SM", [P, NSM, TT, N])
        PR = sb("PR", [P, NSM, TT, N])
        MN = two("MN", [P, H, TT])
        DEN = two("DEN", [P, H, TT])
        RD = two("RD", [P, H, TT])
        RDX = two("RDX", [P, TT, H, HD])
        PT = sb("PT", [P, H, TT, N])
        RS = sb("RS", [P, FC, N])
        OF = two("OF", [P, FC, N])
        OT = two("OT", [P, 2, FC, N], F32R)
        XB = two("XB", [P, TT, D])
        X1 = two("X1", [P, TT, D])
        X1B = two("X1B", [P, TT, D])
        bn2, mv2 = two("bn2", [P, TT, 6]), two("mv2", [P, TT, 2])
        ve2, rs2 = two("ve2", [P, TT]), two("rs2", [P, TT])
        XN2 = two("XN2", [P, TT, D])
        GT = two("GT", [P, 2, FC, N], F32R)
        MJ = two("MJ", [P, 2, TT, D], F32R)
        MIB = two("MIB", [P, TT, D])
        OUT = two("OUT", [P, TT, D])

        S_ps = [ps(f"S_ps_{i}", [P, TT, N]) for i in range(2)]
        PT_ps = [ps(f"PT_ps_{i}", [P, TT, N]) for i in range(2)]
        O_ps = ps("O_ps", [P, FC, N])
        G_ps = [ps(f"G_ps_{i}", [P, 2, N]) for i in range(3)]

        consts_loaded = sem("consts_loaded")
        setup_dve = sem("setup_dve")
        setup_pe = sem("setup_pe")
        setup_pool = sem("setup_pool")
        x_loaded = [sem(f"x_loaded_{i}") for i in range(2)]
        xr_loaded = [sem(f"xr_loaded_{i}") for i in range(2)]
        q_stacked = [sem(f"q_stacked_{i}") for i in range(2)]
        k_stacked = [sem(f"k_stacked_{i}") for i in range(2)]
        stored = [sem(f"stored_{i}") for i in range(2)]
        ht_mm, q_mm, k_mm, v_mm, s_mm, t_mm, o_mm, r_mm, y_mm, gt_mm, mi_mm, mj_mm, a_mm = (
            sem(f"{n}_mm") for n in ("ht", "q", "k", "v", "s", "t", "o", "r", "y", "gt", "mi", "mj", "a"))
        hthi_ok, qhi_ok, khi_ok, v_ok, exp_ok, pt_ok, r_ok, othi_ok, gthi_ok, mjhi_ok = (
            sem(n) for n in ("hthi_ok", "qhi_ok", "khi_ok", "v_ok", "exp_ok", "pt_ok", "r_ok", "othi_ok",
                             "gthi_ok", "mjhi_ok"))
        st1_ok, ht_ok, qlo_ok, klo_ok, min_ok, rd_ok, of_ok, x1_ok, st2_ok, xn2_ok, gt_ok, mj_ok, mib_ok, out_ok = (
            sem(n) for n in ("st1_ok", "ht_ok", "qlo_ok", "klo_ok", "min_ok", "rd_ok", "of_ok", "x1_ok",
                             "st2_ok", "xn2_ok", "gt_ok", "mj_ok", "mib_ok", "out_ok"))
        dve_bn1, dve_mv1, dve_bn2, dve_mv2, dve_rd = (
            sem(n) for n in ("dve_bn1", "dve_mv1", "dve_bn2", "dve_mv2", "dve_rd"))
        dve_passed, pool_passed = sem("dve_passed"), sem("pool_passed")
        rs1_ok, xn1_ok, xb_ok, ot_ok, rs2_ok, x1b_ok = (
            sem(n) for n in ("rs1_ok", "xn1_ok", "xb_ok", "ot_ok", "rs2_ok", "x1b_ok"))
        setup_act = sem("setup_act")

        N_CONST = 14
        SETUP_DVE = 14
        N_STACK = 3
        AHEAD, BEHIND = 3, 3

        def wait(eng, s, value):
            if isinstance(value, int) and value <= 0:
                return
            eng.wait_ge(s, value)

        def stand_alone(eng, passed):
            eng.sem_inc(passed, 1)

        def pipeline(eng, step):
            def at_number(g):
                return lambda k: (g + k, (g + k) // 2, (g + k) % 2) if 0 <= g + k < B else None

            def at_register(i, base):
                return lambda k: (2 * i + (base + k), i + (base + k) // 2, (base + k) % 2)

            first = 5
            pairs = (B - AHEAD - first) // 2
            for g in range(-AHEAD, first):
                step(at_number(g))
            with eng.Fori(0, pairs) as i:
                step(at_register(i, first))
                step(at_register(i, first + 1))
            for g in range(first + 2 * pairs, B + BEHIND):
                step(at_number(g))

        def run(task, graph, *args):
            if graph is not None:
                task(*graph, *args)

        block = ctx.enter_context(nc.Block())

        @block.sync
        def _(sp):
            for tile, src in zip(w_raw, (WqT, WkT, WvT, WoT, WiT, WjT)):
                sp.dma_start(tile[:], src.rearrange("(c p) o -> p c o", p=P)).then_inc(consts_loaded, N_DMA)
            for tile, src in ((bq_raw, bq), (bk_s, bk), (bv_s, bv)):
                sp.dma_start(tile[:], src).then_inc(consts_loaded, N_DMA)
            for tile, src in ((bo_rows, bo), (b1_rows, b1)):
                sp.dma_start(tile[:], src.rearrange("(a f) -> a f", a=1).to_broadcast([P, D])
                             ).then_inc(consts_loaded, N_DMA)
            for tile, src in ((adj_i, adj), (adjT_i, adjT)):
                sp.dma_start(tile[:], src.rearrange("(t p) n -> p t n", p=P)).then_inc(consts_loaded, N_DMA)
            sp.dma_start(idn[:], ident).then_inc(consts_loaded, N_DMA)

            def load_x(n, half, p):
                wait(sp, xn1_ok, n - 1)
                sp.dma_start(X[p][:], x_t[n]).then_inc(x_loaded[p], N_DMA)

            def load_residual(n, half, p):
                wait(sp, x1_ok, n - 1)
                sp.dma_start(XB[p][:], x_t[n]).then_inc(xr_loaded[p], N_DMA)

            def stack(p, stacks, parts, order, stacked):
                for row, part in enumerate(order):
                    sp.dma_start(stacks[p][HD * row:HD * row + HD].rearrange("p a c n -> p (a c n)").bitcast(F32),
                                 parts[:, part].rearrange("p c n -> p (c n)").bitcast(F32)
                                 ).then_inc(stacked[p], N_DMA)

            def stack_q(n, half, p):
                wait(sp, s_mm, H * (n - 1))
                sp.wait_ge(qhi_ok, n + 1)
                sp.wait_ge(qlo_ok, n + 1)
                stack(p, QS, Q, (0, 1, 0), q_stacked)

            def stack_k(n, half, p):
                wait(sp, s_mm, H * (n - 1))
                sp.wait_ge(khi_ok, n + 1)
                sp.wait_ge(klo_ok, n + 1)
                stack(p, KS, K, (0, 0, 1), k_stacked)

            def store(n, half, p):
                sp.wait_ge(out_ok, n + 1)
                sp.dma_start(out_t[n], OUT[p][:]).then_inc(stored[p], N_DMA)

            def step(at):
                run(store, at(-3))
                run(load_x, at(+3))
                run(load_residual, at(0))
                run(stack_q, at(+1))
                run(stack_k, at(+1))

            pipeline(sp, step)
            for i in range(2):
                sp.wait_ge(stored[i], N_DMA * (B // 2))

        @block.gpsimd
        def _(pool):
            pool.memset(minus_half[:], -0.5).then_inc(setup_pool, 1)
            pool.wait_ge(setup_pool, 1)
            pool.wait_ge(setup_dve, SETUP_DVE)

            def norm_1(n, half, p):
                pool.wait_ge(st1_ok, n + 1)
                pool.tensor_tensor(rs1[p][:], ve1[p][:], minus_half[:], ALU.pow).then_inc(rs1_ok, 1)
                pool.wait_ge(rs1_ok, n + 1)
                wait(pool, ht_mm, n - 1)
                stand_alone(pool, pool_passed)
                for t in range(TT):
                    last = pool.tensor_scalar(XN[p][:, t], X[p][:, t], mv1[p][:, t, 0:1], rs1[p][:, t:t + 1],
                                              ALU.subtract, ALU.mult)
                last.then_inc(xn1_ok, 1)

            def add_out_bias(n, half, p):
                pool.wait_ge(xr_loaded[p], N_DMA * (half + 1))
                pool.tensor_tensor(XB[p][:], XB[p][:], out_bias[:], ALU.add).then_inc(xb_ok, 1)

            def attended_lo(n, half, p):
                pool.wait_ge(othi_ok, n + 1)
                pool.tensor_tensor(OT[p][:, 1], OF[p][:], OT[p][:, 0].bitcast(F32), ALU.subtract
                                   ).then_inc(ot_ok, 1)

            def rsqrt_2(n, half, p):
                pool.wait_ge(st2_ok, n + 1)
                pool.tensor_tensor(rs2[p][:], ve2[p][:], minus_half[:], ALU.pow).then_inc(rs2_ok, 1)

            def add_deg_bias(n, half, p):
                pool.wait_ge(x1_ok, n + 1)
                wait(pool, mib_ok, n - 1)
                pool.tensor_tensor(X1B[p][:], X1[p][:], deg_bias[:], ALU.add).then_inc(x1b_ok, 1)

            def step(at):
                run(attended_lo, at(-2))
                run(rsqrt_2, at(-2))
                run(add_out_bias, at(-1))
                run(add_deg_bias, at(-2))
                run(norm_1, at(+2))

            pipeline(pool, step)

        @block.scalar
        def _(act):
            act.wait_ge(consts_loaded, N_DMA * N_CONST)
            for w, raw in zip(weights[1:], w_raw[1:]):
                act.activation(w[:, 0], raw[:], ACT.Copy).then_inc(setup_act, 1)
            act.wait_ge(setup_dve, 2)
            act.activation(wq[:, 0], wq_scaled[:], ACT.Copy).then_inc(setup_act, 1)

            def exps(n, half, p, h):
                act.wait_ge(min_ok, H * n + h + 1)
                wait(act, t_mm, H * n + h + 1 - NSM)
                if h == 0:
                    wait(act, rd_ok, n - 1)
                for t in range(TT):
                    last = act.activation(PR[:, h % NSM, t], SM[:, h % NSM, t], ACT.Exp, scale=-1.0,
                                          bias=MN[p][:, h, t:t + 1], accum_out=DEN[p][:, h, t:t + 1])
                last.then_inc(exp_ok, 1)

            def copy_probs(n, half, p, h):
                if h % HC == 0:
                    wait(act, o_mm, FC * (n - 1) + h // HC + 1)
                act.wait_ge(t_mm, H * n + h + 1)
                act.activation(PT[:, h], PT_ps[h % 2][:], ACT.Copy).then_inc(pt_ok, 1)

            def input_hi(n, half, p):
                act.wait_ge(ht_mm, n + 1)
                wait(act, v_mm, n - 1)
                act.activation(HT[p][:, 0], G_ps[2][:], ACT.Relu).then_inc(hthi_ok, 1)

            def q_hi(n, half, p):
                act.wait_ge(q_mm, n + 1)
                wait(act, q_stacked[1 - p], N_DMA * N_STACK * (half + p))
                for c in range(FC):
                    last = act.activation(Q[:, 0, c], G_ps[1][:, c], ACT.Identity, bias=bq_s[:, c:c + 1])
                last.then_inc(qhi_ok, 1)

            def k_hi(n, half, p):
                act.wait_ge(k_mm, n + 1)
                wait(act, k_stacked[1 - p], N_DMA * N_STACK * (half + p))
                for c in range(FC):
                    last = act.activation(K[:, 0, c], G_ps[0][:, c], ACT.Identity, bias=bk_s[:, c:c + 1])
                last.then_inc(khi_ok, 1)

            def copy_v(n, half, p):
                act.wait_ge(v_mm, n + 1)
                wait(act, o_mm, FC * (n - 1))
                act.activation(V[p][:], G_ps[0][:], ACT.Copy).then_inc(v_ok, 1)

            def copy_denominators(n, half, p):
                act.wait_ge(r_mm, n + 1)
                wait(act, of_ok, n)
                act.activation(RS[:], G_ps[0][:], ACT.Copy).then_inc(r_ok, 1)

            def attended_hi(n, half, p):
                act.wait_ge(of_ok, n + 1)
                wait(act, y_mm, n - 1)
                act.activation(OT[p][:, 0], OF[p][:], ACT.Copy).then_inc(othi_ok, 1)

            def hidden_hi(n, half, p):
                act.wait_ge(gt_mm, n + 1)
                wait(act, mi_mm, n - 1)
                act.activation(GT[p][:, 0], G_ps[2][:], ACT.Relu).then_inc(gthi_ok, 1)

            def neighbours_hi(n, half, p):
                act.wait_ge(mj_mm, n + 1)
                wait(act, a_mm, n - 1)
                act.activation(MJ[p][:, 0], G_ps[2][:], ACT.Copy).then_inc(mjhi_ok, 1)

            def step(at):
                run(exps, at(0), 2)
                run(copy_denominators, at(-1))
                run(q_hi, at(+1))
                run(copy_probs, at(0), 0)
                run(attended_hi, at(-1))
                run(copy_probs, at(0), 1)
                run(k_hi, at(+1))
                run(exps, at(0), 3)
                run(neighbours_hi, at(-2))
                run(exps, at(0), 4)
                run(input_hi, at(+2))
                run(copy_probs, at(0), 2)
                run(exps, at(0), 5)
                run(copy_probs, at(0), 3)
                run(exps, at(0), 6)
                run(copy_probs, at(0), 4)
                run(copy_v, at(+1))
                run(exps, at(0), 7)
                run(copy_probs, at(0), 5)
                run(exps, at(+1), 0)
                run(copy_probs, at(0), 6)
                run(copy_probs, at(0), 7)
                run(exps, at(+1), 1)
                run(hidden_hi, at(-1))

            pipeline(act, step)

        @block.vector
        def _(dve):
            dve.wait_ge(consts_loaded, N_DMA * N_CONST)
            dve.tensor_scalar(wq_scaled[:], w_raw[0][:], -SCALE, None, ALU.mult).then_inc(setup_dve, 1)
            dve.tensor_scalar(bq_s[:], bq_raw[:], -SCALE, None, ALU.mult).then_inc(setup_dve, 1)
            for c in range(FC):
                last = dve.tensor_copy(bv_rep[:, c], bv_s[:, c:c + 1].to_broadcast([P, P]))
            last.then_inc(setup_dve, 1)
            dve.tensor_copy(adj_f[:], adj_i[:]).then_inc(setup_dve, 1)
            dve.tensor_copy(adjT_r[:], adjT_i[:]).then_inc(setup_dve, 1)
            for s in range(2):
                dve.memset(QS[s][3 * HD:].bitcast(F32), 0.0)
                last = dve.memset(KS[s][3 * HD:].bitcast(F32), 0.0)
            last.then_inc(setup_dve, 1)
            dve.wait_ge(setup_dve, 6)
            dve.tensor_scalar(mask[:], adj_f[:], 0.0, MASKED, ALU.is_equal, ALU.mult).then_inc(setup_dve, 1)
            dve.tensor_reduce(deg[:], adj_f[:], AX_X, ALU.add).then_inc(setup_dve, 1)
            dve.wait_ge(setup_dve, 8)
            for n, (w, raw) in enumerate(zip(weights[1:], w_raw[1:])):
                dve.wait_ge(setup_act, n + 1)
                dve.tensor_tensor(w[:, 1], raw[:], w[:, 0].bitcast(F32), ALU.subtract).then_inc(setup_dve, 1)
            dve.wait_ge(setup_act, len(weights))
            dve.tensor_tensor(wq[:, 1], wq_scaled[:], wq[:, 0].bitcast(F32), ALU.subtract)
            dve.wait_ge(setup_pe, 1)
            for t in range(TT):
                dve.tensor_tensor(out_bias[:, t], G_ps[0][:, 0], bo_rows[:], ALU.add)
                last = dve.tensor_scalar(deg_bias[:, t], b1_rows[:], deg[:, t:t + 1], None, ALU.mult)
            last.then_inc(setup_dve, 1)
            dve.wait_ge(setup_dve, SETUP_DVE)

            def row_minima(n, half, p, h):
                dve.wait_ge(s_mm, H * n + h + 1)
                wait(dve, exp_ok, H * n + h + 1 - NSM)
                stand_alone(dve, dve_passed)
                for t in range(TT):
                    last = dve.tensor_tensor_reduce(
                        out=SM[:, h % NSM, t], in0=S_ps[h % 2][:, t], in1=mask[:, t], scale=1.0, scalar=3e38,
                        op0=ALU.add, op1=ALU.min, accum_out=MN[p][:, h, t:t + 1])
                last.then_inc(min_ok, 1)

            def relu_lo(dst, src, ok):
                dve.scalar_tensor_tensor(out=dst[:, 1], in0=src[:], scalar=0.0, in1=dst[:, 0].bitcast(F32),
                                         op0=ALU.max, op1=ALU.subtract).then_inc(ok, 1)

            def biased_lo(dst, src, bias, ok):
                for c in range(FC):
                    last = dve.scalar_tensor_tensor(out=dst[:, 1, c], in0=src[:, c], scalar=bias[:, c:c + 1],
                                                    in1=dst[:, 0, c].bitcast(F32), op0=ALU.add, op1=ALU.subtract)
                last.then_inc(ok, 1)

            def statistics(n, p, src, bn, mv, ve, bn_sem, mv_sem, ok):
                for t in range(TT):
                    last = dve.bn_stats(bn[p][:, t], src[p][:, t])
                last.then_inc(bn_sem, 1)
                dve.wait_ge(bn_sem, n + 1)
                stand_alone(dve, dve_passed)
                for t in range(TT):
                    last = dve.bn_aggr(mv[p][:, t], bn[p][:, t])
                last.then_inc(mv_sem, 1)
                dve.wait_ge(mv_sem, n + 1)
                dve.tensor_scalar(ve[p][:], mv[p][:, :, 1], LN_EPS, None, ALU.add).then_inc(ok, 1)

            def statistics_1(n, half, p):
                dve.wait_ge(x_loaded[p], N_DMA * (half + 1))
                wait(dve, xn1_ok, n - 1)
                statistics(n, p, X, bn1, mv1, ve1, dve_bn1, dve_mv1, st1_ok)

            def input_lo(n, half, p):
                dve.wait_ge(hthi_ok, n + 1)
                relu_lo(HT[p], G_ps[2], ht_ok)

            def q_lo(n, half, p):
                dve.wait_ge(qhi_ok, n + 1)
                biased_lo(Q, G_ps[1], bq_s, qlo_ok)

            def k_lo(n, half, p):
                dve.wait_ge(khi_ok, n + 1)
                biased_lo(K, G_ps[0], bk_s, klo_ok)

            def denominators(n, half, p):
                dve.wait_ge(exp_ok, H * (n + 1))
                dve.reciprocal(RD[p][:], DEN[p][:]).then_inc(dve_rd, 1)
                dve.wait_ge(dve_rd, n + 1)
                wait(dve, r_mm, n - 1)
                for t in range(TT):
                    last = dve.tensor_copy(RDX[p][:, t], RD[p][:, :, t:t + 1].to_broadcast([P, H, HD]))
                last.then_inc(rd_ok, 1)

            def normalise(n, half, p):
                dve.wait_ge(r_ok, n + 1)
                dve.wait_ge(o_mm, FC * (n + 1))
                wait(dve, ot_ok, n - 1)
                dve.tensor_tensor(OF[p][:], O_ps[:], RS[:], ALU.mult).then_inc(of_ok, 1)

            def add_input(n, half, p):
                dve.wait_ge(y_mm, n + 1)
                dve.wait_ge(xb_ok, n + 1)
                wait(dve, x1b_ok, n - 1)
                dve.tensor_tensor(X1[p][:], G_ps[1][:], XB[p][:], ALU.add).then_inc(x1_ok, 1)

            def statistics_2(n, half, p):
                dve.wait_ge(x1_ok, n + 1)
                statistics(n, p, X1, bn2, mv2, ve2, dve_bn2, dve_mv2, st2_ok)

            def norm_2(n, half, p):
                dve.wait_ge(rs2_ok, n + 1)
                wait(dve, gt_mm, n - 1)
                for t in range(TT):
                    last = dve.tensor_scalar(XN2[p][:, t], X1[p][:, t], mv2[p][:, t, 0:1], rs2[p][:, t:t + 1],
                                             ALU.subtract, ALU.mult)
                last.then_inc(xn2_ok, 1)

            def hidden_lo(n, half, p):
                dve.wait_ge(gthi_ok, n + 1)
                relu_lo(GT[p], G_ps[2], gt_ok)

            def neighbours_lo(n, half, p):
                dve.wait_ge(mjhi_ok, n + 1)
                dve.tensor_tensor(MJ[p][:, 1], G_ps[2][:], MJ[p][:, 0].bitcast(F32), ALU.subtract
                                  ).then_inc(mj_ok, 1)

            def add_own(n, half, p):
                dve.wait_ge(mi_mm, n + 1)
                dve.wait_ge(x1b_ok, n + 1)
                for t in range(TT):
                    last = dve.scalar_tensor_tensor(out=MIB[p][:, t], in0=G_ps[1][:, t], scalar=deg[:, t:t + 1],
                                                    in1=X1B[p][:, t], op0=ALU.mult, op1=ALU.add)
                last.then_inc(mib_ok, 1)

            def add_aggregate(n, half, p):
                dve.wait_ge(mib_ok, n + 1)
                dve.wait_ge(a_mm, n + 1)
                wait(dve, stored[p], N_DMA * half)
                dve.tensor_tensor(OUT[p][:], G_ps[2][:], MIB[p][:], ALU.add).then_inc(out_ok, 1)

            def step(at):
                run(statistics_1, at(+2))
                run(row_minima, at(0), 2)
                run(row_minima, at(0), 3)
                run(hidden_lo, at(-2))
                run(row_minima, at(0), 4)
                run(normalise, at(-1))
                run(q_lo, at(+1))
                run(row_minima, at(0), 5)
                run(k_lo, at(+1))
                run(row_minima, at(0), 6)
                run(neighbours_lo, at(-2))
                run(add_input, at(-1))
                run(statistics_2, at(-1))
                run(input_lo, at(+2))
                run(row_minima, at(0), 7)
                run(norm_2, at(-1))
                run(add_own, at(-2))
                run(row_minima, at(+1), 0)
                run(row_minima, at(+1), 1)
                run(denominators, at(0))
                run(add_aggregate, at(-2))

            pipeline(dve, step)

        @block.tensor
        def _(pe):
            pe.wait_ge(consts_loaded, N_DMA * N_CONST)
            pe.wait_ge(setup_dve, 3)
            for c in range(FC):
                last = pe.matmul(G_ps[0][:, 0], bv_rep[:, c], w_raw[3][:, c], start=(c == 0), stop=(c == FC - 1))
            last.then_inc(setup_pe, 1)
            pe.wait_ge(setup_dve, SETUP_DVE)

            HI, LO = 0, 1
            PASSES = ((HI, HI), (HI, LO), (LO, HI))

            def by_feature(dst, w, src, mm):
                for c in range(FC):
                    for n, (k, u, v) in enumerate((k, u, v) for k in range(FC) for u, v in PASSES):
                        last = pe.matmul(dst[:, c], w[:, u, k, P * c:P * c + P], src[:, v, k],
                                         start=(n == 0), stop=(n == FC * len(PASSES) - 1))
                last.then_inc(mm, 1)

            def by_token(dst, src, w, mm):
                for t in range(TT):
                    for n, (k, u, v) in enumerate((k, u, v) for k in range(FC) for u, v in PASSES):
                        last = pe.matmul(dst[:, t], src[:, u, k, P * t:P * t + P], w[:, v, k],
                                         start=(n == 0), stop=(n == FC * len(PASSES) - 1))
                last.then_inc(mm, 1)

            def turn(dst, src, mm):
                for c in range(FC):
                    for t in range(TT):
                        last = pe.transpose(dst[:, c, P * t:P * t + P], src[:, t, P * c:P * c + P], idn[:])
                last.then_inc(mm, 1)

            def bank_read(n, *readers):
                for s, away in readers if isinstance(n, int) else readers[:1]:
                    value = n + away + 1
                    wait(pe, s, min(value, B) if isinstance(n, int) else value)

            def turn_input(n, half, p):
                pe.wait_ge(xn1_ok, n + 1)
                bank_read(n, (mj_ok, -4), (gt_ok, -4), (out_ok, -5), (ht_ok, -1))
                turn(G_ps[2], XN[p], ht_mm)

            def project_q(n, half, p):
                pe.wait_ge(ht_ok, n + 1)
                bank_read(n, (mib_ok, -4), (x1_ok, -3), (qlo_ok, -1))
                by_feature(G_ps[1], wq, HT[p], q_mm)

            def project_k(n, half, p):
                pe.wait_ge(ht_ok, n + 1)
                bank_read(n, (r_ok, -2), (v_ok, -1), (klo_ok, -1))
                by_feature(G_ps[0], wk, HT[p], k_mm)

            def project_v(n, half, p):
                pe.wait_ge(ht_ok, n + 1)
                bank_read(n, (klo_ok, 0), (r_ok, -2), (v_ok, -1))
                by_token(G_ps[0], HT[p], wv, v_mm)

            def scores(n, half, p, h):
                if h == 0:
                    pe.wait_ge(q_stacked[p], N_DMA * N_STACK * (half + 1))
                    pe.wait_ge(k_stacked[p], N_DMA * N_STACK * (half + 1))
                wait(pe, min_ok, H * n + h - 1)
                a, c = h % HC, h // HC
                for t in range(TT):
                    last = pe.matmul(S_ps[h % 2][:, t], QS[p][:, a, c, P * t:P * t + P], KS[p][:, a, c],
                                     start=True, stop=True)
                last.then_inc(s_mm, 1)

            def turn_probs(n, half, p, h):
                pe.wait_ge(exp_ok, H * n + h + 1)
                wait(pe, pt_ok, H * n + h - 1)
                for k in range(TT):
                    for t in range(TT):
                        last = pe.transpose(PT_ps[h % 2][:, k, P * t:P * t + P],
                                            PR[:, h % NSM, t, P * k:P * k + P], idn[:])
                last.then_inc(t_mm, 1)

            def weigh(n, half, p, c):
                pe.wait_ge(pt_ok, H * n + HC * (c + 1))
                if c == 0:
                    pe.wait_ge(v_ok, n + 1)
                    wait(pe, of_ok, n)
                for k in range(TT):
                    for a in range(HC):
                        h = HC * c + a
                        last = pe.matmul(O_ps[HD * a:HD * a + HD, c], V[p][:, k, HD * h:HD * h + HD], PT[:, h, k],
                                         start=(k == 0), stop=(k == TT - 1))
                last.then_inc(o_mm, 1)

            def turn_denominators(n, half, p):
                pe.wait_ge(rd_ok, n + 1)
                bank_read(n, (v_ok, 1), (klo_ok, 1), (r_ok, -1))
                for c in range(FC):
                    for t in range(TT):
                        last = pe.transpose(G_ps[0][:, c, P * t:P * t + P], RDX[p][:, t, HC * c:HC * c + HC], idn[:])
                last.then_inc(r_mm, 1)

            def project_out(n, half, p):
                pe.wait_ge(ot_ok, n + 1)
                bank_read(n, (qlo_ok, 2), (mib_ok, -2), (x1_ok, -1))
                by_token(G_ps[1], OT[p], wo, y_mm)

            def turn_hidden(n, half, p):
                pe.wait_ge(xn2_ok, n + 1)
                bank_read(n, (out_ok, -1), (ht_ok, 3), (mj_ok, -1), (gt_ok, -1))
                turn(G_ps[2], XN2[p], gt_mm)

            def neighbours(n, half, p):
                pe.wait_ge(gt_ok, n + 1)
                bank_read(n, (gt_ok, 0), (out_ok, -1), (ht_ok, 3), (mj_ok, -1))
                by_token(G_ps[2], GT[p], wj, mj_mm)

            def own(n, half, p):
                pe.wait_ge(gt_ok, n + 1)
                bank_read(n, (x1_ok, 1), (qlo_ok, 3), (mib_ok, -1))
                by_token(G_ps[1], GT[p], wi, mi_mm)

            def aggregate(n, half, p):
                pe.wait_ge(mj_ok, n + 1)
                bank_read(n, (ht_ok, 4), (mj_ok, 0), (gt_ok, 0), (out_ok, -1))
                for t in range(TT):
                    for m, (k, v) in enumerate((k, v) for k in range(TT) for v in (HI, LO)):
                        last = pe.matmul(G_ps[2][:, t], adjT_r[:, k, P * t:P * t + P], MJ[p][:, v, k],
                                         start=(m == 0), stop=(m == 2 * TT - 1))
                last.then_inc(a_mm, 1)

            def step(at):
                run(scores, at(0), 3)
                run(turn_probs, at(-1), 7)
                run(weigh, at(-1), 0)
                run(turn_hidden, at(-2))
                run(turn_probs, at(0), 0)
                run(turn_denominators, at(-1))
                run(scores, at(0), 4)
                run(weigh, at(-1), 1)
                run(scores, at(0), 5)
                run(turn_probs, at(0), 1)
                run(project_k, at(+1))
                run(scores, at(0), 6)
                run(neighbours, at(-2))
                run(turn_probs, at(0), 2)
                run(scores, at(0), 7)
                run(project_out, at(-1))
                run(turn_probs, at(0), 3)
                run(turn_input, at(+2))
                run(project_v, at(+1))
                run(turn_probs, at(0), 4)
                run(own, at(-2))
                run(aggregate, at(-2))
                run(scores, at(+1), 0)
                run(turn_probs, at(0), 5)
                run(scores, at(+1), 1)
                run(project_q, at(+2))
                run(turn_probs, at(0), 6)
                run(scores, at(+1), 2)

            pipeline(pe, step)


def kernel(x, adj, L0_gnn_Wq, L0_gnn_bq, L0_gnn_Wk, L0_gnn_bk, L0_gnn_Wv, L0_gnn_bv, L0_gnn_Wo, L0_gnn_bo,
           L1_gnn_W, L1_gnn_b):
    import numpy as np
    import concourse.bacc as bacc
    from concourse.bass_utils import run_bass_kernel_spmd

    def laid(a):
        return np.ascontiguousarray(np.asarray(a))

    D = x.shape[2]
    W1 = np.asarray(L1_gnn_W)

    def by_partition(b):
        return laid(np.asarray(b).reshape(D // P, P).T)

    def dims_first(w):
        w = np.asarray(w)
        return laid(w.reshape(D // P, P // 32, 32, -1).transpose(0, 2, 1, 3).reshape(w.shape))

    arrays = {
        "x": laid(x),
        "WqT": laid(dims_first(L0_gnn_Wq).T), "WkT": laid(dims_first(L0_gnn_Wk).T),
        "WvT": laid(np.asarray(L0_gnn_Wv).T), "WoT": laid(np.asarray(L0_gnn_Wo).T),
        "WiT": laid(W1[:, :D].T), "WjT": laid(W1[:, D:].T),
        "bq": by_partition(dims_first(L0_gnn_bq)), "bk": by_partition(dims_first(L0_gnn_bk)), "bv": by_partition(L0_gnn_bv),
        "bo": laid(L0_gnn_bo), "b1": laid(L1_gnn_b),
        "adj": laid(adj), "adjT": laid(np.asarray(adj).T),
        "ident": np.eye(P, dtype=np.float32),
    }
    nc = bacc.Bacc("TRN2", target_bir_lowering=False, num_devices=1)
    args = [nc.dram_tensor(f"in_{n}", a.shape, mybir.dt.from_np(a.dtype), kind="ExternalInput").ap()
            for n, a in arrays.items()]
    out = nc.dram_tensor("out", x.shape, F32, kind="ExternalOutput").ap()
    graph_layers(nc, *args, out)
    r = run_bass_kernel_spmd(nc, [{f"in_{n}": a for n, a in arrays.items()}], core_ids=[0])
    return r.results[0]["out"]
```

```python
from contextlib import ExitStack

import concourse.bass as bass
from concourse import mybir

F32 = mybir.dt.float32
F32R = mybir.dt.float32r
I32 = mybir.dt.int32
ALU = mybir.AluOpType
ACT = mybir.ActivationFunctionType
AX_X = mybir.AxisListType.X

P = 128
LN_EPS = 1e-5
MASKED = 1e30
N_DMA = 16


def graph_layers(nc, x, qk_weights, other_weights, biases, bias_rows, adjacency, ident, out):
    B, N, D = x.shape
    TT = N // P
    FC = D // P
    HD = 32
    H = D // HD
    HC = P // HD
    SCALE = float(HD) ** -0.5
    assert TT == 2 and FC == 2 and N == 256 and D == 256

    x_t = x.rearrange("b (t p) f -> b p t f", p=P)
    out_t = out.rearrange("b (t p) f -> b p t f", p=P)

    with ExitStack() as ctx:
        def sb(name, shape, dt=F32):
            return ctx.enter_context(nc.sbuf_tensor(name, shape, dt))

        def ps(name, shape):
            return ctx.enter_context(nc.psum_tensor(name, shape, F32))

        def sem(name):
            return ctx.enter_context(nc.semaphore(name))

        qk_raw = sb("qk_raw", [P, 2 * FC, D])
        other_raw = sb("other_raw", [P, 4 * FC, D])
        wq_raw, wk_raw = (qk_raw[:, FC * i:FC * i + FC] for i in range(2))
        wv_raw, wo_raw, wi_raw, wj_raw = (other_raw[:, FC * i:FC * i + FC] for i in range(4))
        weights = [sb(f"w_{n}", [P, 2, FC, D], F32R) for n in ("q", "k", "v", "o", "i", "j")]
        wq, wk, wv, wo, wi, wj = weights
        wq_scaled = sb("wq_scaled", [P, FC, D])
        bias_cols = sb("bias_cols", [P, 3 * FC])
        bq_raw, bk_s, bv_s = (bias_cols[:, FC * i:FC * i + FC] for i in range(3))
        bq_s = sb("bq_s", [P, FC])
        bv_rep = sb("bv_rep", [P, FC, P])
        bo_b1_rows = sb("bo_b1_rows", [P, 2 * D])
        bo_rows, b1_rows = (bo_b1_rows[:, D * i:D * i + D] for i in range(2))
        adj_both = sb("adj_both", [P, 2 * TT, N], I32)
        adj_i, adjT_i = (adj_both[:, TT * i:TT * i + TT] for i in range(2))
        adj_f = sb("adj_f", [P, TT, N])
        adjT_r = sb("adjT_r", [P, TT, N], F32R)
        mask = sb("mask", [P, TT, N])
        deg = sb("deg", [P, TT])
        out_bias = sb("out_bias", [P, TT, D])
        deg_bias = sb("deg_bias", [P, TT, D])
        idn = sb("idn", [P, P])
        minus_half = sb("minus_half", [P, TT])
        zeros = sb("zeros", [P, P])

        def two(name, shape, dt=F32):
            return [sb(f"{name}_{i}", shape, dt) for i in range(2)]

        X = two("X", [P, TT, D])
        bn1, mv1 = two("bn1", [P, TT, 6]), two("mv1", [P, TT, 2])
        ve1, rs1 = two("ve1", [P, TT]), two("rs1", [P, TT])
        XN = two("XN", [P, TT, D])
        HT = two("HT", [P, 2, FC, N], F32R)
        Q = sb("Q", [P, 2, FC, N], F32R)
        K = sb("K", [P, 2, FC, N], F32R)
        QS = two("QS", [P, HC, FC, N], F32R)
        KS = two("KS", [P, HC, FC, N], F32R)
        V = two("V", [P, TT, D])
        NSM = 4
        SM = sb("SM", [P, NSM, TT, N])
        PR = sb("PR", [P, NSM, TT, N])
        MN = two("MN", [P, H, TT])
        DEN = two("DEN", [P, H, TT])
        RD = two("RD", [P, H, TT])
        RDX = two("RDX", [P, TT, H, HD])
        PT = sb("PT", [P, H, TT, N])
        RS = sb("RS", [P, FC, N])
        OF = two("OF", [P, FC, N])
        OT = two("OT", [P, 2, FC, N], F32R)
        XB = two("XB", [P, TT, D])
        X1 = two("X1", [P, TT, D])
        X1B = two("X1B", [P, TT, D])
        bn2, mv2 = two("bn2", [P, TT, 6]), two("mv2", [P, TT, 2])
        ve2, rs2 = two("ve2", [P, TT]), two("rs2", [P, TT])
        XN2 = two("XN2", [P, TT, D])
        GT = two("GT", [P, 2, FC, N], F32R)
        MJ = two("MJ", [P, 2, TT, D], F32R)
        MIB = two("MIB", [P, TT, D])
        OUT = two("OUT", [P, TT, D])

        S_ps = [ps(f"S_ps_{i}", [P, TT, N]) for i in range(2)]
        PT_ps = [ps(f"PT_ps_{i}", [P, TT, N]) for i in range(2)]
        O_ps = ps("O_ps", [P, FC, N])
        G_ps = [ps(f"G_ps_{i}", [P, 2, N]) for i in range(3)]

        qk_loaded, adj_loaded, ident_loaded, rest_loaded = (
            sem(n) for n in ("qk_loaded", "adj_loaded", "ident_loaded", "rest_loaded"))
        setup_dve = sem("setup_dve")
        hi_ok, split_ok = sem("hi_ok"), sem("split_ok")
        setup_act = sem("setup_act")
        wo_bv_mm = sem("wo_bv_mm")
        zeros_set = sem("zeros_set")
        setup_pool = sem("setup_pool")
        x_loaded = [sem(f"x_loaded_{i}") for i in range(2)]
        xr_loaded = [sem(f"xr_loaded_{i}") for i in range(2)]
        q_stacked = [sem(f"q_stacked_{i}") for i in range(2)]
        k_stacked = [sem(f"k_stacked_{i}") for i in range(2)]
        stored = [sem(f"stored_{i}") for i in range(2)]
        ht_mm, q_mm, k_mm, v_mm, s_mm, t_mm, o_mm, r_mm, y_mm, gt_mm, mi_mm, mj_mm, a_mm = (
            sem(f"{n}_mm") for n in ("ht", "q", "k", "v", "s", "t", "o", "r", "y", "gt", "mi", "mj", "a"))
        hthi_ok, qhi_ok, khi_ok, v_ok, exp_ok, pt_ok, r_ok, othi_ok, gthi_ok, mjhi_ok = (
            sem(n) for n in ("hthi_ok", "qhi_ok", "khi_ok", "v_ok", "exp_ok", "pt_ok", "r_ok", "othi_ok",
                             "gthi_ok", "mjhi_ok"))
        st1_ok, ht_ok, qlo_ok, klo_ok, min_ok, rd_ok, of_ok, x1_ok, st2_ok, xn2_ok, gt_ok, mj_ok, mib_ok, out_ok = (
            sem(n) for n in ("st1_ok", "ht_ok", "qlo_ok", "klo_ok", "min_ok", "rd_ok", "of_ok", "x1_ok",
                             "st2_ok", "xn2_ok", "gt_ok", "mj_ok", "mib_ok", "out_ok"))
        dve_bn1, dve_mv1, dve_bn2, dve_mv2, dve_rd = (
            sem(n) for n in ("dve_bn1", "dve_mv1", "dve_bn2", "dve_mv2", "dve_rd"))
        dve_passed, pool_passed = sem("dve_passed"), sem("pool_passed")
        rs1_ok, xn1_ok, xb_ok, ot_ok, rs2_ok, x1b_ok = (
            sem(n) for n in ("rs1_ok", "xn1_ok", "xb_ok", "ot_ok", "rs2_ok", "x1b_ok"))

        SETUP_DVE = 9
        SETUP_POOL = 3
        WARM_UP = 24
        N_STACK = 3
        AHEAD, BEHIND = 3, 3

        def wait(eng, s, value):
            if isinstance(value, int) and value <= 0:
                return
            eng.wait_ge(s, value)

        def stand_alone(eng, passed):
            eng.sem_inc(passed, 1)

        def pipeline(eng, step):
            def at_number(g):
                return lambda k: (g + k, (g + k) // 2, (g + k) % 2) if 0 <= g + k < B else None

            def at_register(i, base):
                return lambda k: (2 * i + (base + k), i + (base + k) // 2, (base + k) % 2)

            first = 5
            pairs = (B - AHEAD - first) // 2
            for g in range(-AHEAD, first):
                step(at_number(g))
            with eng.Fori(0, pairs) as i:
                step(at_register(i, first))
                step(at_register(i, first + 1))
            for g in range(first + 2 * pairs, B + BEHIND):
                step(at_number(g))

        def run(task, graph, *args):
            if graph is not None:
                task(*graph, *args)

        def is_first(n):
            return isinstance(n, int) and n == 0

        def is_early(n):
            return isinstance(n, int) and n < 2

        block = ctx.enter_context(nc.Block())

        @block.sync
        def _(sp):
            def load_x(n, half, p, early=False):
                if is_early(n) and not early:
                    return
                wait(sp, xn1_ok, n - 1)
                sp.dma_start(X[p][:], x_t[n]).then_inc(x_loaded[p], N_DMA)

            load_x(0, 0, 0, early=True)
            sp.dma_start(qk_raw[:], qk_weights.rearrange("(c p) o -> p c o", p=P)).then_inc(qk_loaded, N_DMA)
            sp.dma_start(bias_cols[:], biases).then_inc(qk_loaded, N_DMA)
            load_x(1, 0, 1, early=True)
            sp.dma_start(idn[:], ident).then_inc(ident_loaded, N_DMA)
            sp.dma_start(adj_both[:], adjacency.rearrange("(t p) n -> p t n", p=P)).then_inc(adj_loaded, N_DMA)
            sp.dma_start(other_raw[:], other_weights.rearrange("(c p) o -> p c o", p=P)
                         ).then_inc(rest_loaded, N_DMA)
            sp.dma_start(bo_b1_rows[:], bias_rows.rearrange("(a f) -> a f", a=1).to_broadcast([P, 2 * D])
                         ).then_inc(rest_loaded, N_DMA)

            def load_residual(n, half, p):
                wait(sp, x1_ok, n - 1)
                sp.dma_start(XB[p][:], x_t[n]).then_inc(xr_loaded[p], N_DMA)

            def stack(p, stacks, parts, order, stacked):
                for row, part in enumerate(order):
                    sp.dma_start(stacks[p][HD * row:HD * row + HD].rearrange("p a c n -> p (a c n)").bitcast(F32),
                                 parts[:, part].rearrange("p c n -> p (c n)").bitcast(F32)
                                 ).then_inc(stacked[p], N_DMA)

            def stack_q(n, half, p):
                wait(sp, s_mm, H * (n - 1))
                sp.wait_ge(qhi_ok, n + 1)
                sp.wait_ge(qlo_ok, n + 1)
                stack(p, QS, Q, (0, 1, 0), q_stacked)

            def stack_k(n, half, p):
                wait(sp, s_mm, H * (n - 1))
                sp.wait_ge(khi_ok, n + 1)
                sp.wait_ge(klo_ok, n + 1)
                stack(p, KS, K, (0, 0, 1), k_stacked)

            def store(n, half, p):
                sp.wait_ge(out_ok, n + 1)
                sp.dma_start(out_t[n], OUT[p][:]).then_inc(stored[p], N_DMA)

            def step(at):
                run(store, at(-3))
                run(load_x, at(+3))
                run(stack_q, at(+1))
                run(load_residual, at(0))
                run(stack_k, at(+1))

            pipeline(sp, step)
            for i in range(2):
                sp.wait_ge(stored[i], N_DMA * (B // 2))

        @block.gpsimd
        def _(pool):
            pool.memset(minus_half[:], -0.5).then_inc(setup_pool, 1)
            for n, stack in enumerate((KS[0], QS[1])):
                pool.wait_ge(setup_pool, n + 1)
                pool.memset(stack[3 * HD:].bitcast(F32), 0.0).then_inc(setup_pool, 1)
            pool.wait_ge(setup_pool, SETUP_POOL)

            def norm_1(n, half, p):
                pool.wait_ge(st1_ok, n + 1)
                pool.tensor_tensor(rs1[p][:], ve1[p][:], minus_half[:], ALU.pow).then_inc(rs1_ok, 1)
                pool.wait_ge(rs1_ok, n + 1)
                wait(pool, ht_mm, n - 1)
                stand_alone(pool, pool_passed)
                for t in range(TT):
                    last = pool.tensor_scalar(XN[p][:, t], X[p][:, t], mv1[p][:, t, 0:1], rs1[p][:, t:t + 1],
                                              ALU.subtract, ALU.mult)
                last.then_inc(xn1_ok, 1)

            def add_out_bias(n, half, p):
                if is_first(n):
                    pool.wait_ge(setup_dve, SETUP_DVE)
                pool.wait_ge(xr_loaded[p], N_DMA * (half + 1))
                pool.tensor_tensor(XB[p][:], XB[p][:], out_bias[:], ALU.add).then_inc(xb_ok, 1)

            def attended_lo(n, half, p):
                pool.wait_ge(othi_ok, n + 1)
                pool.tensor_tensor(OT[p][:, 1], OF[p][:], OT[p][:, 0].bitcast(F32), ALU.subtract
                                   ).then_inc(ot_ok, 1)

            def rsqrt_2(n, half, p):
                pool.wait_ge(st2_ok, n + 1)
                pool.tensor_tensor(rs2[p][:], ve2[p][:], minus_half[:], ALU.pow).then_inc(rs2_ok, 1)

            def add_deg_bias(n, half, p):
                pool.wait_ge(x1_ok, n + 1)
                wait(pool, mib_ok, n - 1)
                pool.tensor_tensor(X1B[p][:], X1[p][:], deg_bias[:], ALU.add).then_inc(x1b_ok, 1)

            def step(at):
                run(rsqrt_2, at(-2))
                run(add_deg_bias, at(-2))
                run(add_out_bias, at(-1))
                run(norm_1, at(+2))
                run(attended_lo, at(-1))

            pipeline(pool, step)

        @block.scalar
        def _(act):
            act.wait_ge(setup_pool, 2)
            act.activation(KS[1][3 * HD:], KS[0][3 * HD:].bitcast(F32), ACT.Copy).then_inc(setup_act, 1)
            act.wait_ge(qk_loaded, N_DMA * 2)
            act.activation(wk[:, 0], wk_raw, ACT.Copy).then_inc(hi_ok, 1)
            act.wait_ge(setup_dve, 3)
            act.activation(wq[:, 0], wq_scaled[:], ACT.Copy).then_inc(hi_ok, 1)

            def other_weights_hi():
                act.wait_ge(rest_loaded, N_DMA * 2)
                for w, raw in ((wv, wv_raw), (wo, wo_raw), (wi, wi_raw), (wj, wj_raw)):
                    act.activation(w[:, 0], raw, ACT.Copy).then_inc(hi_ok, 1)

            def exps(n, half, p, h):
                act.wait_ge(min_ok, H * n + h + 1)
                wait(act, t_mm, H * n + h + 1 - NSM)
                if h == 0:
                    wait(act, rd_ok, n - 1)
                for t in range(TT):
                    last = act.activation(PR[:, h % NSM, t], SM[:, h % NSM, t], ACT.Exp, scale=-1.0,
                                          bias=MN[p][:, h, t:t + 1], accum_out=DEN[p][:, h, t:t + 1])
                last.then_inc(exp_ok, 1)

            def copy_probs(n, half, p, h):
                if h % HC == 0:
                    wait(act, o_mm, FC * (n - 1) + h // HC + 1)
                act.wait_ge(t_mm, H * n + h + 1)
                act.activation(PT[:, h], PT_ps[h % 2][:], ACT.Copy).then_inc(pt_ok, 1)

            def input_hi(n, half, p):
                act.wait_ge(ht_mm, n + 1)
                wait(act, v_mm, n - 1)
                act.activation(HT[p][:, 0], G_ps[2][:], ACT.Relu).then_inc(hthi_ok, 1)
                if is_first(n):
                    other_weights_hi()

            def q_hi(n, half, p):
                act.wait_ge(q_mm, n + 1)
                wait(act, q_stacked[1 - p], N_DMA * N_STACK * (half + p))
                for c in range(FC):
                    last = act.activation(Q[:, 0, c], G_ps[1][:, c], ACT.Identity, bias=bq_s[:, c:c + 1])
                last.then_inc(qhi_ok, 1)

            def k_hi(n, half, p):
                act.wait_ge(k_mm, n + 1)
                wait(act, k_stacked[1 - p], N_DMA * N_STACK * (half + p))
                for c in range(FC):
                    last = act.activation(K[:, 0, c], G_ps[0][:, c], ACT.Identity, bias=bk_s[:, c:c + 1])
                last.then_inc(khi_ok, 1)

            def copy_v(n, half, p):
                act.wait_ge(v_mm, n + 1)
                wait(act, o_mm, FC * (n - 1))
                act.activation(V[p][:], G_ps[0][:], ACT.Copy).then_inc(v_ok, 1)

            def copy_denominators(n, half, p):
                act.wait_ge(r_mm, n + 1)
                wait(act, of_ok, n)
                act.activation(RS[:], G_ps[0][:], ACT.Copy).then_inc(r_ok, 1)

            def attended_hi(n, half, p):
                act.wait_ge(of_ok, n + 1)
                wait(act, y_mm, n - 1)
                act.activation(OT[p][:, 0], OF[p][:], ACT.Copy).then_inc(othi_ok, 1)

            def hidden_hi(n, half, p):
                act.wait_ge(gt_mm, n + 1)
                wait(act, mi_mm, n - 1)
                act.activation(GT[p][:, 0], G_ps[2][:], ACT.Relu).then_inc(gthi_ok, 1)

            def neighbours_hi(n, half, p):
                act.wait_ge(mj_mm, n + 1)
                wait(act, a_mm, n - 1)
                act.activation(MJ[p][:, 0], G_ps[2][:], ACT.Copy).then_inc(mjhi_ok, 1)

            def step(at):
                run(exps, at(0), 2)
                run(copy_denominators, at(-1))
                run(q_hi, at(+1))
                run(copy_probs, at(0), 0)
                run(attended_hi, at(-1))
                run(copy_probs, at(0), 1)
                run(k_hi, at(+1))
                run(exps, at(0), 3)
                run(neighbours_hi, at(-2))
                run(exps, at(0), 4)
                run(copy_probs, at(0), 2)
                run(exps, at(0), 5)
                run(input_hi, at(+2))
                run(copy_probs, at(0), 3)
                run(exps, at(0), 6)
                run(copy_v, at(+1))
                run(copy_probs, at(0), 4)
                run(exps, at(0), 7)
                run(copy_probs, at(0), 5)
                run(exps, at(+1), 0)
                run(copy_probs, at(0), 6)
                run(copy_probs, at(0), 7)
                run(exps, at(+1), 1)
                run(hidden_hi, at(-1))

            pipeline(act, step)

        @block.vector
        def _(dve):
            def row_minima(n, half, p, h):
                dve.wait_ge(s_mm, H * n + h + 1)
                wait(dve, exp_ok, H * n + h + 1 - NSM)
                stand_alone(dve, dve_passed)
                for t in range(TT):
                    last = dve.tensor_tensor_reduce(
                        out=SM[:, h % NSM, t], in0=S_ps[h % 2][:, t], in1=mask[:, t], scale=1.0, scalar=3e38,
                        op0=ALU.add, op1=ALU.min, accum_out=MN[p][:, h, t:t + 1])
                last.then_inc(min_ok, 1)

            def relu_lo(dst, src, ok):
                dve.scalar_tensor_tensor(out=dst[:, 1], in0=src[:], scalar=0.0, in1=dst[:, 0].bitcast(F32),
                                         op0=ALU.max, op1=ALU.subtract).then_inc(ok, 1)

            def biased_lo(dst, src, bias, ok):
                for c in range(FC):
                    last = dve.scalar_tensor_tensor(out=dst[:, 1, c], in0=src[:, c], scalar=bias[:, c:c + 1],
                                                    in1=dst[:, 0, c].bitcast(F32), op0=ALU.add, op1=ALU.subtract)
                last.then_inc(ok, 1)

            def statistics(n, p, src, bn, mv, ve, bn_sem, mv_sem, ok):
                for t in range(TT):
                    last = dve.bn_stats(bn[p][:, t], src[p][:, t])
                last.then_inc(bn_sem, 1)
                dve.wait_ge(bn_sem, n + 1)
                stand_alone(dve, dve_passed)
                for t in range(TT):
                    last = dve.bn_aggr(mv[p][:, t], bn[p][:, t])
                last.then_inc(mv_sem, 1)
                dve.wait_ge(mv_sem, n + 1)
                dve.tensor_scalar(ve[p][:], mv[p][:, :, 1], LN_EPS, None, ALU.add).then_inc(ok, 1)

            def statistics_1(n, half, p, early=False):
                if is_early(n) and not early:
                    return
                dve.wait_ge(x_loaded[p], N_DMA * (half + 1))
                wait(dve, xn1_ok, n - 1)
                statistics(n, p, X, bn1, mv1, ve1, dve_bn1, dve_mv1, st1_ok)

            dve.memset(zeros[:], 0.0).then_inc(zeros_set, 1)
            dve.memset(QS[0][3 * HD:].bitcast(F32), 0.0).then_inc(setup_dve, 1)
            statistics_1(0, 0, 0, early=True)
            dve.wait_ge(qk_loaded, N_DMA * 2)
            dve.tensor_scalar(bq_s[:], bq_raw, -SCALE, None, ALU.mult).then_inc(setup_dve, 1)
            dve.tensor_scalar(wq_scaled[:], wq_raw, -SCALE, None, ALU.mult).then_inc(setup_dve, 1)
            for c in range(FC):
                last = dve.tensor_copy(bv_rep[:, c], bv_s[:, c:c + 1].to_broadcast([P, P]))
            last.then_inc(setup_dve, 1)
            dve.wait_ge(hi_ok, 1)
            dve.tensor_tensor(wk[:, 1], wk_raw, wk[:, 0].bitcast(F32), ALU.subtract).then_inc(split_ok, 1)
            dve.wait_ge(hi_ok, 2)
            dve.wait_ge(setup_dve, 3)
            dve.tensor_tensor(wq[:, 1], wq_scaled[:], wq[:, 0].bitcast(F32), ALU.subtract).then_inc(split_ok, 1)
            statistics_1(1, 0, 1, early=True)
            dve.wait_ge(adj_loaded, N_DMA)
            dve.tensor_copy(adj_f[:], adj_i).then_inc(setup_dve, 1)
            dve.tensor_copy(adjT_r[:], adjT_i).then_inc(setup_dve, 1)
            dve.wait_ge(setup_dve, 5)
            dve.tensor_scalar(mask[:], adj_f[:], 0.0, MASKED, ALU.is_equal, ALU.mult).then_inc(setup_dve, 1)
            dve.tensor_reduce(deg[:], adj_f[:], AX_X, ALU.add).then_inc(setup_dve, 1)

            def other_weights_lo():
                for n, (w, raw) in enumerate(((wv, wv_raw), (wo, wo_raw), (wi, wi_raw), (wj, wj_raw))):
                    dve.wait_ge(hi_ok, n + 3)
                    dve.tensor_tensor(w[:, 1], raw, w[:, 0].bitcast(F32), ALU.subtract).then_inc(split_ok, 1)
                dve.wait_ge(rest_loaded, N_DMA * 2)
                dve.wait_ge(setup_dve, 8)
                for t in range(TT):
                    dve.tensor_scalar(deg_bias[:, t], b1_rows, deg[:, t:t + 1], None, ALU.mult)
                dve.wait_ge(wo_bv_mm, 1)
                for t in range(TT):
                    last = dve.tensor_tensor(out_bias[:, t], O_ps[:, 0], bo_rows, ALU.add)
                last.then_inc(setup_dve, 1)
                dve.wait_ge(setup_dve, SETUP_DVE)

            def input_lo(n, half, p):
                dve.wait_ge(hthi_ok, n + 1)
                relu_lo(HT[p], G_ps[2], ht_ok)
                if isinstance(n, int) and n == 1:
                    other_weights_lo()

            def q_lo(n, half, p):
                dve.wait_ge(qhi_ok, n + 1)
                biased_lo(Q, G_ps[1], bq_s, qlo_ok)

            def k_lo(n, half, p):
                dve.wait_ge(khi_ok, n + 1)
                biased_lo(K, G_ps[0], bk_s, klo_ok)

            def denominators(n, half, p):
                dve.wait_ge(exp_ok, H * (n + 1))
                dve.reciprocal(RD[p][:], DEN[p][:]).then_inc(dve_rd, 1)
                dve.wait_ge(dve_rd, n + 1)
                wait(dve, r_mm, n - 1)
                for t in range(TT):
                    last = dve.tensor_copy(RDX[p][:, t], RD[p][:, :, t:t + 1].to_broadcast([P, H, HD]))
                last.then_inc(rd_ok, 1)

            def normalise(n, half, p):
                dve.wait_ge(r_ok, n + 1)
                dve.wait_ge(o_mm, FC * (n + 1))
                wait(dve, ot_ok, n - 1)
                dve.tensor_tensor(OF[p][:], O_ps[:], RS[:], ALU.mult).then_inc(of_ok, 1)

            def add_input(n, half, p):
                dve.wait_ge(y_mm, n + 1)
                dve.wait_ge(xb_ok, n + 1)
                wait(dve, x1b_ok, n - 1)
                dve.tensor_tensor(X1[p][:], G_ps[1][:], XB[p][:], ALU.add).then_inc(x1_ok, 1)

            def statistics_2(n, half, p):
                dve.wait_ge(x1_ok, n + 1)
                statistics(n, p, X1, bn2, mv2, ve2, dve_bn2, dve_mv2, st2_ok)

            def norm_2(n, half, p):
                dve.wait_ge(rs2_ok, n + 1)
                wait(dve, gt_mm, n - 1)
                for t in range(TT):
                    last = dve.tensor_scalar(XN2[p][:, t], X1[p][:, t], mv2[p][:, t, 0:1], rs2[p][:, t:t + 1],
                                             ALU.subtract, ALU.mult)
                last.then_inc(xn2_ok, 1)

            def hidden_lo(n, half, p):
                dve.wait_ge(gthi_ok, n + 1)
                relu_lo(GT[p], G_ps[2], gt_ok)

            def neighbours_lo(n, half, p):
                dve.wait_ge(mjhi_ok, n + 1)
                dve.tensor_tensor(MJ[p][:, 1], G_ps[2][:], MJ[p][:, 0].bitcast(F32), ALU.subtract
                                  ).then_inc(mj_ok, 1)

            def add_own(n, half, p):
                dve.wait_ge(mi_mm, n + 1)
                dve.wait_ge(x1b_ok, n + 1)
                for t in range(TT):
                    last = dve.scalar_tensor_tensor(out=MIB[p][:, t], in0=G_ps[1][:, t], scalar=deg[:, t:t + 1],
                                                    in1=X1B[p][:, t], op0=ALU.mult, op1=ALU.add)
                last.then_inc(mib_ok, 1)

            def add_aggregate(n, half, p):
                dve.wait_ge(mib_ok, n + 1)
                dve.wait_ge(a_mm, n + 1)
                wait(dve, stored[p], N_DMA * half)
                dve.tensor_tensor(OUT[p][:], G_ps[0][:], MIB[p][:], ALU.add).then_inc(out_ok, 1)

            def step(at):
                run(statistics_1, at(+2))
                run(row_minima, at(0), 2)
                run(row_minima, at(0), 3)
                run(hidden_lo, at(-2))
                run(row_minima, at(0), 4)
                run(normalise, at(-1))
                run(q_lo, at(+1))
                run(row_minima, at(0), 5)
                run(k_lo, at(+1))
                run(row_minima, at(0), 6)
                run(neighbours_lo, at(-2))
                run(add_input, at(-1))
                run(statistics_2, at(-1))
                run(input_lo, at(+2))
                run(row_minima, at(0), 7)
                run(norm_2, at(-1))
                run(add_own, at(-2))
                run(row_minima, at(+1), 0)
                run(row_minima, at(+1), 1)
                run(add_aggregate, at(-2))
                run(denominators, at(0))

            pipeline(dve, step)

        @block.tensor
        def _(pe):
            pe.wait_ge(zeros_set, 1)
            for _ in range(WARM_UP):
                pe.matmul(O_ps[:, 1, :P], zeros[:], zeros[:], start=True, stop=True)
            pe.wait_ge(ident_loaded, N_DMA)

            HI, LO = 0, 1
            PASSES = ((HI, HI), (HI, LO), (LO, HI))

            def by_feature(dst, w, src, mm):
                for c in range(FC):
                    for n, (k, u, v) in enumerate((k, u, v) for k in range(FC) for u, v in PASSES):
                        last = pe.matmul(dst[:, c], w[:, u, k, P * c:P * c + P], src[:, v, k],
                                         start=(n == 0), stop=(n == FC * len(PASSES) - 1))
                last.then_inc(mm, 1)

            def by_token(dst, src, w, mm):
                for t in range(TT):
                    for n, (k, u, v) in enumerate((k, u, v) for k in range(FC) for u, v in PASSES):
                        last = pe.matmul(dst[:, t], src[:, u, k, P * t:P * t + P], w[:, v, k],
                                         start=(n == 0), stop=(n == FC * len(PASSES) - 1))
                last.then_inc(mm, 1)

            def turn(dst, src, mm):
                for c in range(FC):
                    for t in range(TT):
                        last = pe.transpose(dst[:, c, P * t:P * t + P], src[:, t, P * c:P * c + P], idn[:])
                last.then_inc(mm, 1)

            def bank_read(n, *readers):
                for s, away in readers if isinstance(n, int) else readers[:1]:
                    value = n + away + 1
                    wait(pe, s, min(value, B) if isinstance(n, int) else value)

            def project_v_bias():
                pe.wait_ge(rest_loaded, N_DMA * 2)
                pe.wait_ge(setup_dve, 4)
                for c in range(FC):
                    last = pe.matmul(O_ps[:, 0], bv_rep[:, c], wo_raw[:, c], start=(c == 0), stop=(c == FC - 1))
                last.then_inc(wo_bv_mm, 1)

            def turn_input(n, half, p):
                pe.wait_ge(xn1_ok, n + 1)
                bank_read(n, (mj_ok, -4), (gt_ok, -4), (ht_ok, -1))
                turn(G_ps[2], XN[p], ht_mm)

            def project_q(n, half, p):
                if is_first(n):
                    pe.wait_ge(split_ok, 2)
                pe.wait_ge(ht_ok, n + 1)
                bank_read(n, (mib_ok, -4), (x1_ok, -3), (qlo_ok, -1))
                by_feature(G_ps[1], wq, HT[p], q_mm)

            def project_k(n, half, p):
                if is_first(n):
                    pe.wait_ge(split_ok, 1)
                pe.wait_ge(ht_ok, n + 1)
                bank_read(n, (r_ok, -2), (out_ok, -4), (v_ok, -1), (klo_ok, -1))
                by_feature(G_ps[0], wk, HT[p], k_mm)

            def project_v(n, half, p):
                if is_first(n):
                    project_v_bias()
                    pe.wait_ge(split_ok, 3)
                pe.wait_ge(ht_ok, n + 1)
                bank_read(n, (klo_ok, 0), (r_ok, -2), (out_ok, -4), (v_ok, -1))
                by_token(G_ps[0], HT[p], wv, v_mm)

            def scores(n, half, p, h):
                if is_first(n) and h == 0:
                    pe.wait_ge(setup_dve, SETUP_DVE)
                    pe.wait_ge(setup_pool, SETUP_POOL)
                    pe.wait_ge(setup_act, 1)
                if h == 0:
                    pe.wait_ge(q_stacked[p], N_DMA * N_STACK * (half + 1))
                    pe.wait_ge(k_stacked[p], N_DMA * N_STACK * (half + 1))
                wait(pe, min_ok, H * n + h - 1)
                a, c = h % HC, h // HC
                for t in range(TT):
                    last = pe.matmul(S_ps[h % 2][:, t], QS[p][:, a, c, P * t:P * t + P], KS[p][:, a, c],
                                     start=True, stop=True)
                last.then_inc(s_mm, 1)

            def turn_probs(n, half, p, h):
                pe.wait_ge(exp_ok, H * n + h + 1)
                wait(pe, pt_ok, H * n + h - 1)
                for k in range(TT):
                    for t in range(TT):
                        last = pe.transpose(PT_ps[h % 2][:, k, P * t:P * t + P],
                                            PR[:, h % NSM, t, P * k:P * k + P], idn[:])
                last.then_inc(t_mm, 1)

            def weigh(n, half, p, c):
                pe.wait_ge(pt_ok, H * n + HC * (c + 1))
                if c == 0:
                    pe.wait_ge(v_ok, n + 1)
                    wait(pe, of_ok, n)
                for k in range(TT):
                    for a in range(HC):
                        h = HC * c + a
                        last = pe.matmul(O_ps[HD * a:HD * a + HD, c], V[p][:, k, HD * h:HD * h + HD], PT[:, h, k],
                                         start=(k == 0), stop=(k == TT - 1))
                last.then_inc(o_mm, 1)

            def turn_denominators(n, half, p):
                pe.wait_ge(rd_ok, n + 1)
                bank_read(n, (out_ok, -2), (v_ok, 1), (klo_ok, 1), (r_ok, -1))
                for c in range(FC):
                    for t in range(TT):
                        last = pe.transpose(G_ps[0][:, c, P * t:P * t + P], RDX[p][:, t, HC * c:HC * c + HC], idn[:])
                last.then_inc(r_mm, 1)

            def project_out(n, half, p):
                pe.wait_ge(ot_ok, n + 1)
                bank_read(n, (qlo_ok, 2), (mib_ok, -2), (x1_ok, -1))
                by_token(G_ps[1], OT[p], wo, y_mm)

            def turn_hidden(n, half, p):
                pe.wait_ge(xn2_ok, n + 1)
                bank_read(n, (ht_ok, 3), (mj_ok, -1), (gt_ok, -1))
                turn(G_ps[2], XN2[p], gt_mm)

            def neighbours(n, half, p):
                pe.wait_ge(gt_ok, n + 1)
                bank_read(n, (gt_ok, 0), (ht_ok, 3), (mj_ok, -1))
                by_token(G_ps[2], GT[p], wj, mj_mm)

            def own(n, half, p):
                pe.wait_ge(gt_ok, n + 1)
                bank_read(n, (x1_ok, 1), (qlo_ok, 3), (mib_ok, -1))
                by_token(G_ps[1], GT[p], wi, mi_mm)

            def aggregate(n, half, p):
                pe.wait_ge(mj_ok, n + 1)
                bank_read(n, (v_ok, 3), (klo_ok, 3), (r_ok, 1), (out_ok, -1))
                for t in range(TT):
                    for m, (k, v) in enumerate((k, v) for k in range(TT) for v in (HI, LO)):
                        last = pe.matmul(G_ps[0][:, t], adjT_r[:, k, P * t:P * t + P], MJ[p][:, v, k],
                                         start=(m == 0), stop=(m == 2 * TT - 1))
                last.then_inc(a_mm, 1)

            def step(at):
                run(scores, at(0), 2)
                run(scores, at(0), 3)
                run(turn_probs, at(-1), 6)
                run(turn_probs, at(-1), 7)
                run(weigh, at(-1), 0)
                run(turn_hidden, at(-2))
                run(turn_probs, at(0), 0)
                run(turn_denominators, at(-1))
                run(scores, at(0), 4)
                run(weigh, at(-1), 1)
                run(scores, at(0), 5)
                run(turn_probs, at(0), 1)
                run(project_k, at(+1))
                run(neighbours, at(-2))
                run(scores, at(0), 6)
                run(turn_probs, at(0), 2)
                run(scores, at(0), 7)
                run(project_out, at(-1))
                run(turn_input, at(+2))
                run(turn_probs, at(0), 3)
                run(turn_probs, at(0), 4)
                run(project_v, at(+1))
                run(own, at(-2))
                run(scores, at(+1), 0)
                run(aggregate, at(-2))
                run(turn_probs, at(0), 5)
                run(scores, at(+1), 1)
                run(project_q, at(+2))

            pipeline(pe, step)


def kernel(x, adj, L0_gnn_Wq, L0_gnn_bq, L0_gnn_Wk, L0_gnn_bk, L0_gnn_Wv, L0_gnn_bv, L0_gnn_Wo, L0_gnn_bo,
           L1_gnn_W, L1_gnn_b):
    import numpy as np
    import concourse.bacc as bacc
    from concourse.bass_utils import run_bass_kernel_spmd

    def laid(a):
        return np.ascontiguousarray(np.asarray(a))

    D = x.shape[2]
    W1 = np.asarray(L1_gnn_W)

    def by_partition(b):
        return laid(np.asarray(b).reshape(D // P, P).T)

    def dims_first(w):
        w = np.asarray(w)
        return laid(w.reshape(D // P, P // 32, 32, -1).transpose(0, 2, 1, 3).reshape(w.shape))

    arrays = {
        "x": laid(x),
        "qk_weights": laid(np.concatenate([dims_first(L0_gnn_Wq).T, dims_first(L0_gnn_Wk).T])),
        "other_weights": laid(np.concatenate([np.asarray(L0_gnn_Wv).T, np.asarray(L0_gnn_Wo).T,
                                              W1[:, :D].T, W1[:, D:].T])),
        "biases": laid(np.concatenate([by_partition(b) for b in (dims_first(L0_gnn_bq), dims_first(L0_gnn_bk),
                                                                 L0_gnn_bv)], axis=1)),
        "bias_rows": laid(np.concatenate([np.asarray(L0_gnn_bo), np.asarray(L1_gnn_b)])),
        "adjacency": laid(np.concatenate([np.asarray(adj), np.asarray(adj).T])),
        "ident": np.eye(P, dtype=np.float32),
    }
    nc = bacc.Bacc("TRN2", target_bir_lowering=False, num_devices=1)
    args = [nc.dram_tensor(f"in_{n}", a.shape, mybir.dt.from_np(a.dtype), kind="ExternalInput").ap()
            for n, a in arrays.items()]
    out = nc.dram_tensor("out", x.shape, F32, kind="ExternalOutput").ap()
    graph_layers(nc, *args, out)
    r = run_bass_kernel_spmd(nc, [{f"in_{n}": a for n, a in arrays.items()}], core_ids=[0])
    return r.results[0]["out"]
```
